# Optimizing a Trainium2 kernel written in Bass

```python
import numpy as np
import jax
import jax.numpy as jnp

def _softmax(x, axis=-1):
    return jax.nn.softmax(x, axis=axis)

def _gelu(x):
    return jax.nn.gelu(x, approximate=True)

def _silu(x):
    return jax.nn.silu(x)

def _sigmoid(x):
    return jax.nn.sigmoid(x)

def _layernorm(x, axis=-1, eps=1e-05):
    m = jnp.mean(x, axis=axis, keepdims=True)
    v = jnp.var(x, axis=axis, keepdims=True)
    return (x - m) / jnp.sqrt(v + eps)

def _scatter_add(tgt, idx, src, axis=0):
    return tgt.at[idx].add(src)

def _segment_sum(src, seg, n):
    return jax.ops.segment_sum(src, seg, n)
kernel_name = 'mk_early_fusion_d1_tok_img1024_r4_6f1664'

def setup_inputs(seed: int=0):
    np.random.seed(seed)
    _w = jnp.asarray

    def _rec_inputs():
        import jax
        import jax.numpy as jnp
        _rk = jax.random.key(seed)
        x = -0.000125008 + 0.999885 * jax.random.normal(jax.random.fold_in(_rk, 1), (16, 512, 256, 4), jnp.float32)
        txt = -8.03667e-05 + 0.656214 * jax.random.normal(jax.random.fold_in(_rk, 2), (16, 128, 256), jnp.float32)
        return (x, txt)
    x, txt = _rec_inputs()

    def _L0_tok_setup():
        import jax, jax.numpy as jnp
        import numpy as np
        key = jax.random.key(seed)
        k1, k2, k3 = jax.random.split(key, 3)
        B, H, I, O, Dp1 = (4, 512, 256, 256, 4)
        x = jax.random.normal(k1, (B, H, I, Dp1), dtype=jnp.float32)
        weight = 0.1 * jax.random.normal(k2, (O, Dp1), dtype=jnp.float32)
        weighted_sum = 0.1 * jax.random.normal(k3, (O, I), dtype=jnp.float32)
        return {'x': x, 'weight': weight, 'weighted_sum': weighted_sum}
    _L0_tok_all = _L0_tok_setup()
    _L0_tok_in = {k: v for k, v in _L0_tok_all.items() if k in ('weight', 'weighted_sum')}
    del _L0_tok_all

    def _L0_attn_setup():
        import jax, jax.numpy as jnp
        import numpy as np
        import math
        D_MODEL = 256
        NUM_HEADS = 16
        D_K = D_MODEL // NUM_HEADS
        B, S = (4, 512)
        key = jax.random.key(seed)
        ks = jax.random.split(key, 9)
        sc = 1.0 / math.sqrt(D_MODEL)
        return {'x': jax.random.normal(ks[0], (B, S, D_MODEL), jnp.float32), 'Wq': jax.random.normal(ks[1], (D_MODEL, D_MODEL), jnp.float32) * sc, 'bq': jax.random.normal(ks[2], (D_MODEL,), jnp.float32) * 0.01, 'Wk': jax.random.normal(ks[3], (D_MODEL, D_MODEL), jnp.float32) * sc, 'bk': jax.random.normal(ks[4], (D_MODEL,), jnp.float32) * 0.01, 'Wv': jax.random.normal(ks[5], (D_MODEL, D_MODEL), jnp.float32) * sc, 'bv': jax.random.normal(ks[6], (D_MODEL,), jnp.float32) * 0.01, 'Wo': jax.random.normal(ks[7], (D_MODEL, D_MODEL), jnp.float32) * sc, 'bo': jax.random.normal(ks[8], (D_MODEL,), jnp.float32) * 0.01}
    _L0_attn_all = _L0_attn_setup()
    _L0_attn_in = {k: v for k, v in _L0_attn_all.items() if k in ('Wq', 'bq', 'Wk', 'bk', 'Wv', 'bv', 'Wo', 'bo')}
    del _L0_attn_all

    def _L0_ffn_setup():
        import jax, jax.numpy as jnp
        import numpy as np
        B, T, C, H, E, MIN_E = (4, 512, 256, 128, 16, 2)
        IS_CAUSAL = False

        def _forward(hidden_states, sim_matrix, gates, q_proj, k_proj, v_proj, o_proj):
            b, t, c = hidden_states.shape
            n = b * t
            x = hidden_states.reshape(n, c)
            xn = x / jnp.maximum(jnp.linalg.norm(x, axis=-1, keepdims=True), 1e-12)
            sn = sim_matrix / jnp.maximum(jnp.linalg.norm(sim_matrix, axis=0, keepdims=True), 1e-12)
            logits = xn @ sn - jax.nn.sigmoid(gates)
            gated = jax.nn.relu(logits)
            hard = (gated > 0).astype(gated.dtype)
            mask = gated + jax.lax.stop_gradient(hard - gated)
            inactive = jnp.sum(hard, axis=1) == 0
            _, fb_idx = jax.lax.top_k(logits, MIN_E)
            fb = jnp.zeros((n, logits.shape[1]), gated.dtype).at[jnp.arange(n)[:, None], fb_idx].set(1.0)
            put = jax.lax.stop_gradient(inactive[:, None].astype(gated.dtype) * fb)
            mask = mask * (1.0 - put) + put
            masked = jnp.where(mask > 0, gated, -jnp.inf)
            w = jax.nn.softmax(masked, axis=-1)

            def moe_proj(p):
                y = jnp.einsum('nc,ech->neh', x, p)
                return jnp.einsum('ne,neh->nh', w, y)
            q = moe_proj(q_proj).reshape(b, t, -1)
            k = moe_proj(k_proj).reshape(b, t, -1)
            v = moe_proj(v_proj).reshape(b, t, -1)
            h = q.shape[-1]
            scores = jnp.einsum('bth,bsh->bts', q, k) / jnp.sqrt(jnp.asarray(h, q.dtype))
            if IS_CAUSAL and t > 1:
                causal = jnp.tril(jnp.ones((t, t), bool))
                scores = jnp.where(causal[None], scores, -jnp.inf)
            attn = jax.nn.softmax(scores, axis=-1)
            o = jnp.einsum('bts,bsh->bth', attn, v).reshape(n, h)
            z = jnp.einsum('ne,nh->enh', w, o)
            out = jnp.einsum('enh,ehc->nc', z, o_proj)
            return out.reshape(b, t, c)
        key = jax.random.key(seed)
        ks = jax.random.split(key, 6)
        lim_qkv = float(np.sqrt(6.0 / (C + H)))
        inp = {'hidden_states': jax.random.normal(ks[0], (B, T, C), jnp.float32), 'sim_matrix': jax.random.normal(ks[1], (C, E), jnp.float32), 'gates': jnp.zeros((E,), jnp.float32), 'q_proj': jax.random.uniform(ks[2], (E, C, H), jnp.float32, -lim_qkv, lim_qkv), 'k_proj': jax.random.uniform(ks[3], (E, C, H), jnp.float32, -lim_qkv, lim_qkv), 'v_proj': jax.random.uniform(ks[4], (E, C, H), jnp.float32, -lim_qkv, lim_qkv), 'o_proj': jax.random.uniform(ks[5], (E, H, C), jnp.float32, -lim_qkv, lim_qkv)}
        return inp
    _L0_ffn_all = _L0_ffn_setup()
    _L0_ffn_in = {k: v for k, v in _L0_ffn_all.items() if k in ('sim_matrix', 'gates', 'q_proj', 'k_proj', 'v_proj', 'o_proj')}
    del _L0_ffn_all
    return {'x': x, 'txt': txt, 'L0_tok_weight': _L0_tok_in['weight'], 'L0_tok_weighted_sum': _L0_tok_in['weighted_sum'], 'L0_attn_Wq': _L0_attn_in['Wq'], 'L0_attn_bq': _L0_attn_in['bq'], 'L0_attn_Wk': _L0_attn_in['Wk'], 'L0_attn_bk': _L0_attn_in['bk'], 'L0_attn_Wv': _L0_attn_in['Wv'], 'L0_attn_bv': _L0_attn_in['bv'], 'L0_attn_Wo': _L0_attn_in['Wo'], 'L0_attn_bo': _L0_attn_in['bo'], 'L0_ffn_sim_matrix': _L0_ffn_in['sim_matrix'], 'L0_ffn_gates': _L0_ffn_in['gates'], 'L0_ffn_q_proj': _L0_ffn_in['q_proj'], 'L0_ffn_k_proj': _L0_ffn_in['k_proj'], 'L0_ffn_v_proj': _L0_ffn_in['v_proj'], 'L0_ffn_o_proj': _L0_ffn_in['o_proj']}

def reference(x, txt, L0_tok_weight, L0_tok_weighted_sum, L0_attn_Wq, L0_attn_bq, L0_attn_Wk, L0_attn_bk, L0_attn_Wv, L0_attn_bv, L0_attn_Wo, L0_attn_bo, L0_ffn_sim_matrix, L0_ffn_gates, L0_ffn_q_proj, L0_ffn_k_proj, L0_ffn_v_proj, L0_ffn_o_proj):
    import jax
    import jax.numpy as jnp

    def _L0_tok_ref(x, weight, weighted_sum):
        import jax, jax.numpy as jnp
        import numpy as np
        return jnp.einsum('bhid,oi,od->bho', x, weighted_sum, weight)

    def _L0_attn_ref(x, Wq, bq, Wk, bk, Wv, bv, Wo, bo):
        import jax, jax.numpy as jnp
        import numpy as np
        import math
        D_MODEL = 256
        NUM_HEADS = 16
        D_K = D_MODEL // NUM_HEADS
        B, S = (4, 512)
        b, s, d = x.shape
        Q = x @ Wq.T + bq
        K = x @ Wk.T + bk
        V = x @ Wv.T + bv
        split = lambda t: t.reshape(b, s, NUM_HEADS, D_K).transpose(0, 2, 1, 3)
        Q, K, V = (split(Q), split(K), split(V))
        seq = jnp.arange(s)
        causal = seq[:, None] >= seq[None, :]
        scores = jnp.einsum('bhqd,bhkd->bhqk', Q, K) / math.sqrt(D_K)
        scores = jnp.where(causal, scores, -jnp.inf)
        weights = jax.nn.softmax(scores, axis=-1)
        attn = jnp.einsum('bhqk,bhkd->bhqd', weights, V)
        attn = attn.transpose(0, 2, 1, 3).reshape(b, s, NUM_HEADS * D_K)
        return attn @ Wo.T + bo

    def _L0_ffn_ref(hidden_states, sim_matrix, gates, q_proj, k_proj, v_proj, o_proj):
        import jax, jax.numpy as jnp
        import numpy as np
        B, T, C, H, E, MIN_E = (4, 512, 256, 128, 16, 2)
        IS_CAUSAL = False

        def _forward(hidden_states, sim_matrix, gates, q_proj, k_proj, v_proj, o_proj):
            b, t, c = hidden_states.shape
            n = b * t
            x = hidden_states.reshape(n, c)
            xn = x / jnp.maximum(jnp.linalg.norm(x, axis=-1, keepdims=True), 1e-12)
            sn = sim_matrix / jnp.maximum(jnp.linalg.norm(sim_matrix, axis=0, keepdims=True), 1e-12)
            logits = xn @ sn - jax.nn.sigmoid(gates)
            gated = jax.nn.relu(logits)
            hard = (gated > 0).astype(gated.dtype)
            mask = gated + jax.lax.stop_gradient(hard - gated)
            inactive = jnp.sum(hard, axis=1) == 0
            _, fb_idx = jax.lax.top_k(logits, MIN_E)
            fb = jnp.zeros((n, logits.shape[1]), gated.dtype).at[jnp.arange(n)[:, None], fb_idx].set(1.0)
            put = jax.lax.stop_gradient(inactive[:, None].astype(gated.dtype) * fb)
            mask = mask * (1.0 - put) + put
            masked = jnp.where(mask > 0, gated, -jnp.inf)
            w = jax.nn.softmax(masked, axis=-1)

            def moe_proj(p):
                y = jnp.einsum('nc,ech->neh', x, p)
                return jnp.einsum('ne,neh->nh', w, y)
            q = moe_proj(q_proj).reshape(b, t, -1)
            k = moe_proj(k_proj).reshape(b, t, -1)
            v = moe_proj(v_proj).reshape(b, t, -1)
            h = q.shape[-1]
            scores = jnp.einsum('bth,bsh->bts', q, k) / jnp.sqrt(jnp.asarray(h, q.dtype))
            if IS_CAUSAL and t > 1:
                causal = jnp.tril(jnp.ones((t, t), bool))
                scores = jnp.where(causal[None], scores, -jnp.inf)
            attn = jax.nn.softmax(scores, axis=-1)
            o = jnp.einsum('bts,bsh->bth', attn, v).reshape(n, h)
            z = jnp.einsum('ne,nh->enh', w, o)
            out = jnp.einsum('enh,ehc->nc', z, o_proj)
            return out.reshape(b, t, c)
        return _forward(hidden_states, sim_matrix, gates, q_proj, k_proj, v_proj, o_proj)
    h = _L0_tok_ref(x, L0_tok_weight, L0_tok_weighted_sum)
    h = jnp.concatenate([h, txt], axis=1)
    h = h + _L0_attn_ref(_layernorm(h, axis=-1), L0_attn_Wq, L0_attn_bq, L0_attn_Wk, L0_attn_bk, L0_attn_Wv, L0_attn_bv, L0_attn_Wo, L0_attn_bo)
    h = h + _L0_ffn_ref(_layernorm(h, axis=-1), L0_ffn_sim_matrix, L0_ffn_gates, L0_ffn_q_proj, L0_ffn_k_proj, L0_ffn_v_proj, L0_ffn_o_proj)
    return h

_drawn_inputs = setup_inputs


def setup_inputs(seed=0):
    import zlib

    import numpy as np

    out = dict(_drawn_inputs(seed))
    spreads = {'L0_ffn_gates': (0.0, 0.1)}
    factors = {'L0_attn_bq': 7.727, 'L0_attn_bk': 8.0}
    for name, (base, spread) in spreads.items():
        noise = np.random.default_rng([zlib.crc32(name.encode()), seed]).standard_normal(out[name].shape)
        drawn = base * np.exp(spread * noise) if base else spread * noise
        out[name] = jnp.asarray(drawn.astype(out[name].dtype))
    for name, factor in factors.items():
        out[name] = (out[name] * factor).astype(out[name].dtype)
    return out
```

```python
import concourse.bass as bass
from concourse import mybir
from contextlib import ExitStack

F32 = mybir.dt.float32
F32R = mybir.dt.float32r
BF16 = mybir.dt.bfloat16
ALU = mybir.AluOpType
ACT = mybir.ActivationFunctionType
AX = mybir.AxisListType

P = 128
B = 16
T_IMG, T_TXT = 512, 128
T = T_IMG + T_TXT
NT = T // P
C = 256
NC = C // P
XD = 4
KX = C * XD // P
HALF = T // 2
HEADS, DK = 16, 16
HPC = P // DK
PARTS = 3
EPS = 1e-5
MASKED = -1e30
BANK = 512


def front_phase(nc, a, scratch):
    ctx = ExitStack()
    with ctx:
        def sb(name, shape, dt=F32):
            return ctx.enter_context(nc.sbuf_tensor(name, shape, dt))

        def sem(name):
            return ctx.enter_context(nc.semaphore(name))

        stage_ws = sb("a_stage_ws", [P, KX, C])
        stage_w = sb("a_stage_w", [P, KX, C])
        tok_hi = sb("a_tok_hi", [P, KX, C], F32R)
        tok_lo = sb("a_tok_lo", [P, KX, C], F32R)
        stage_qkv = sb("a_stage_qkv", [P, 3, NC, C])
        qkv_hi = sb("a_qkv_hi", [P, 3, NC, C], F32R)
        qkv_lo = sb("a_qkv_lo", [P, 3, NC, C], F32R)
        bias_in = sb("a_bias_in", [P, 2, NC])
        bias_qk = sb("a_bias_qk", [P, 2, NC])
        ident = sb("a_ident", [P, P])
        x_in = sb("a_x_in", [P, 2, KX, T_IMG])
        x_hi = sb("a_x_hi", [P, KX, T_IMG], F32R)
        x_lo = sb("a_x_lo", [P, KX, T_IMG], F32R)
        h = sb("a_h", [P, 2, NT, C])
        stats = sb("a_stats", [P, NT, 6])
        mean_sum = sb("a_mean_sum", [P, NT, 2])
        mean_diff = sb("a_mean_diff", [P, NT, 1])
        mean = sb("a_mean", [P, NT, 1])
        spread = sb("a_spread", [P, NT, 1])
        var_eps = sb("a_var_eps", [P, NT, 1])
        minus_half = sb("a_minus_half", [P, NT, 1])
        var = sb("a_var", [P, NT, 1])
        rstd = sb("a_rstd", [P, NT, 1])
        xn = sb("a_xn", [P, NT, C])
        xt_hi = sb("a_xt_hi", [P, NC, T], F32R)
        xt_lo = sb("a_xt_lo", [P, NC, T], F32R)
        qk = sb("a_qk", [P, 4, T])
        rest = sb("a_rest", [P, 4, T])
        pieces = sb("a_pieces", [P, 2, 4, PARTS, T], BF16)
        v_out = sb("a_v_out", [P, 2, NT, C])

        tok_ps = ctx.enter_context(nc.psum_tensor("a_tok_ps", [P, 2, BANK], F32))
        xt_ps = ctx.enter_context(nc.psum_tensor("a_xt_ps", [P, 3 * BANK], F32))
        ring_ps = ctx.enter_context(nc.psum_tensor("a_ring_ps", [P, 3, BANK], F32))

        loaded = sem("a_loaded")
        w_made = sem("a_w_made")
        ones_set = sem("a_ones_set")
        x_loaded = [sem(f"a_x_loaded{s}") for s in range(2)]
        x_high = sem("a_x_high")
        x_low = sem("a_x_low")
        tok_done = sem("a_tok_done")
        h_copied = sem("a_h_copied")
        txt_loaded = [sem(f"a_txt_loaded{s}") for s in range(2)]
        st_done = sem("a_st_done")
        ag_done = sem("a_ag_done")
        var_done = sem("a_var_done")
        rstd_done = sem("a_rstd_done")
        xn_done = sem("a_xn_done")
        xt_done = sem("a_xt_done")
        xt_high = sem("a_xt_high")
        xt_low = sem("a_xt_low")
        ring_qk = sem("a_ring_qk")
        qk_out = sem("a_qk_out")
        ring_v = sem("a_ring_v")
        v_copied = sem("a_v_copied")
        part1 = sem("a_part1")
        rest1 = sem("a_rest1")
        part2 = sem("a_part2")
        part3 = sem("a_part3")
        h_stored = sem("a_h_stored")
        stored = sem("a_stored")
        out_free = sem("a_out_free")

        STORES = 2
        tok_src = a["x_t"].rearrange("b (k p) t -> b p k t", p=P)
        block = ctx.enter_context(nc.Block())

        def loads(b, s):
            return 8 * (b - s) + 16

        def load_x(sp, b, s):
            sp.dma_start(x_in[:, s], tok_src[b]).then_inc(x_loaded[s], 16)

        @block.sync
        def _(sp):
            for dst, src in ((stage_ws[:], a["ws_rep"].rearrange("(k p) o -> p k o", p=P)),
                             (stage_w[:], a["w_rep"].rearrange("(k p) o -> p k o", p=P)),
                             (stage_qkv[:], a["w_qkv"].rearrange("j (c p) o -> p j c o", p=P)),
                             (bias_in[:], a["b_qk"]), (ident[:], a["ident"])):
                sp.dma_start(dst, src).then_inc(loaded, 16)
            for b in range(2):
                load_x(sp, b, b)
            sp.dma_start(h[:, 0, NT - 1, :], a["txt"][0]).then_inc(txt_loaded[0], 16)
            sp.dma_start(h[:, 1, NT - 1, :], a["txt"][1]).then_inc(txt_loaded[1], 16)

            sp.wait_ge(x_low, 4)
            load_x(sp, 2, 0)

            def step(b, s, more, load):
                sp.wait_ge(stored, 16 * STORES * b)
                sp.sem_inc(out_free, 1)
                if load:
                    sp.wait_ge(x_low, 4 * (b + 2))
                    load_x(sp, b + 3, 1 - s)
                sp.wait_ge(h_copied, 4 * (b + 1))
                sp.wait_ge(txt_loaded[s], loads(b, s))
                sp.dma_start(scratch["h"][b], h[:, s]).then_inc(h_stored, 16)
                sp.wait_ge(v_copied, NT * (b + 1))
                sp.dma_start(scratch["v"][b], v_out[:, s]).then_inc(stored, 16)
                if more:
                    sp.wait_ge(h_stored, 16 * (b + 1))
                    sp.wait_ge(xn_done, NT * (b + 1))
                    sp.dma_start(h[:, s, NT - 1, :], a["txt"][b + 2]).then_inc(txt_loaded[s], 16)
                sp.wait_ge(part1, 4 * (b + 1))
                sp.wait_ge(part2, 4 * (b + 1))
                sp.wait_ge(part3, 4 * (b + 1))
                sp.dma_start(scratch["pieces"][b], pieces[:, s]).then_inc(stored, 16)

            for s in range(2):
                step(s, s, True, True)
            with sp.Fori(1, B // 2 - 2) as i:
                for s in range(2):
                    step(2 * i + s, s, True, True)
            for b in range(B - 4, B):
                step(b, b % 2, b + 2 < B, b + 3 < B)
            sp.wait_ge(h_stored, 16 * B)
            sp.wait_ge(stored, 16 * STORES * B)

        @block.scalar
        def _(act):
            act.wait_ge(w_made, 4)

            def h_out(b, s):
                act.wait_ge(txt_loaded[s], loads(b, s))
                for t in range(4):
                    act.wait_ge(tok_done, 4 * b + t + 1)
                    nc.scalar.copy(h[:, s, t, :], tok_ps[:, t % 2, 0:C]).then_inc(h_copied, 1)

            def transposed(b):
                act.wait_ge(xt_done, b + 1)
                nc.scalar.copy(xt_hi[:].rearrange("p c t -> p (c t)"), xt_ps[:, 0:NC * T]).then_inc(xt_high, 1)

            def project(b, s):
                act.wait_ge(part3, 4 * b)
                act.wait_ge(out_free, b)
                for u in range(4):
                    for half in range(2):
                        n = 2 * u + half
                        act.wait_ge(ring_qk, 8 * b + n + 1)
                        nc.scalar.activation(qk[:, u, half * HALF:(half + 1) * HALF], ring_ps[:, n % 3, 0:HALF],
                                             ACT.Identity, bias=bias_qk[:, u // 2, u % 2:u % 2 + 1],
                                             scale=0.25 if u < 2 else 1.0).then_inc(qk_out, 1)
                    act.wait_ge(qk_out, 8 * b + 2 * u + 2)
                    nc.scalar.copy(pieces[:, s, u, 0], qk[:, u]).then_inc(part1, 1)
                for u in range(4):
                    act.wait_ge(rest1, 4 * b + u + 1)
                    nc.scalar.copy(pieces[:, s, u, 1], rest[:, u]).then_inc(part2, 1)

            h_out(0, 0)

            def step(b, s, more):
                transposed(b)
                if more:
                    h_out(b + 1, 1 - s)
                project(b, s)

            for s in range(2):
                step(s, s, True)
            with act.Fori(1, B // 2 - 1) as i:
                for s in range(2):
                    step(2 * i + s, s, True)
            step(B - 2, 0, True)
            step(B - 1, 1, False)

        @block.vector
        def _(dve):
            dve.wait_ge(loaded, 16 * 5)
            nc.vector.tensor_tensor(stage_ws[:], stage_ws[:], stage_w[:], ALU.mult).then_inc(w_made, 1)
            nc.vector.tensor_copy(qkv_hi[:], stage_qkv[:]).then_inc(w_made, 1)
            nc.vector.tensor_copy(bias_qk[:, 1], bias_in[:, 1]).then_inc(w_made, 1)
            nc.vector.tensor_scalar(bias_qk[:, 0], bias_in[:, 0], 0.25, None, ALU.mult).then_inc(w_made, 1)
            dve.wait_ge(w_made, 4)
            nc.vector.tensor_copy(tok_hi[:], stage_ws[:]).then_inc(w_made, 1)
            nc.vector.tensor_tensor(qkv_lo[:], stage_qkv[:], qkv_hi[:].bitcast(F32), ALU.subtract).then_inc(w_made, 1)
            dve.wait_ge(w_made, 6)
            nc.vector.tensor_tensor(tok_lo[:], stage_ws[:], tok_hi[:].bitcast(F32), ALU.subtract).then_inc(w_made, 1)

            def split(b, s, t):
                rows = slice(t * P, (t + 1) * P)
                if t == 0:
                    dve.wait_ge(x_loaded[s], loads(b, s))
                nc.vector.tensor_copy(x_hi[:, :, rows], x_in[:, s, :, rows]).then_inc(x_high, 1)
                dve.wait_ge(x_high, 4 * b + t + 1)
                nc.vector.tensor_tensor(x_lo[:, :, rows], x_in[:, s, :, rows], x_hi[:, :, rows].bitcast(F32),
                                        ALU.subtract).then_inc(x_low, 1)

            def norm(b, s, ahead):
                dve.wait_ge(xt_done, b)
                for t in range(NT):
                    if t < NT - 1:
                        dve.wait_ge(h_copied, 4 * b + t + 1)
                    else:
                        dve.wait_ge(txt_loaded[s], loads(b, s))
                    nc.vector.bn_stats(stats[:, t], h[:, s, t]).then_inc(st_done, 1)
                    if ahead and t < NT - 1:
                        split(b + 1, 1 - s, t)
                dve.wait_ge(st_done, NT * (b + 1))
                even, odd = stats[:, :, 0:3], stats[:, :, 3:6]
                nc.vector.tensor_tensor(mean_sum[:], even[:, :, 1:3], odd[:, :, 1:3], ALU.add).then_inc(ag_done, 1)
                nc.vector.tensor_tensor(mean_diff[:], even[:, :, 1:2], odd[:, :, 1:2], ALU.subtract).then_inc(ag_done, 1)
                dve.wait_ge(ag_done, 5 * b + 2)
                nc.vector.tensor_scalar(mean[:], mean_sum[:, :, 0:1], 0.5, None, ALU.mult).then_inc(ag_done, 1)
                nc.vector.scalar_tensor_tensor(out=spread[:], in0=mean_diff[:], scalar=0.25, in1=mean_diff[:],
                                               op0=ALU.mult, op1=ALU.mult).then_inc(ag_done, 1)
                dve.wait_ge(ag_done, 5 * b + 4)
                nc.vector.scalar_tensor_tensor(out=var[:], in0=mean_sum[:, :, 1:2], scalar=1.0 / C, in1=spread[:],
                                               op0=ALU.mult, op1=ALU.add).then_inc(ag_done, 1)
                dve.wait_ge(ag_done, 5 * b + 5)
                nc.vector.tensor_scalar(var_eps[:], var[:], EPS, None, ALU.add).then_inc(var_done, 1)
                dve.wait_ge(rstd_done, b + 1)
                for t in range(NT):
                    nc.vector.tensor_scalar(xn[:, t], h[:, s, t], mean[:, t, 0:1], rstd[:, t, 0:1],
                                            ALU.subtract, ALU.mult).then_inc(xn_done, 1)

            def transposed(b):
                dve.wait_ge(xt_high, b + 1)
                nc.vector.tensor_tensor(xt_lo[:].rearrange("p c t -> p (c t)"), xt_ps[:, 0:NC * T],
                                        xt_hi[:].rearrange("p c t -> p (c t)").bitcast(F32), ALU.subtract).then_inc(xt_low, 1)

            def values(b, s):
                dve.wait_ge(out_free, b)
                for t in range(NT):
                    dve.wait_ge(ring_v, NT * b + t + 1)
                    nc.vector.tensor_copy(v_out[:, s, t], ring_ps[:, (8 + t) % 3, 0:C]).then_inc(v_copied, 1)

            for t in range(NT - 1):
                split(0, 0, t)
            norm(0, 0, True)

            def step(b, s, ahead):
                transposed(b)
                if ahead >= 1:
                    norm(b + 1, 1 - s, ahead >= 2)
                values(b, s)

            for s in range(2):
                step(s, s, 2)
            with dve.Fori(1, B // 2 - 1) as i:
                for s in range(2):
                    step(2 * i + s, s, 2)
            step(B - 2, 0, 1)
            step(B - 1, 1, 0)

        @block.gpsimd
        def _(pool):
            def inverse_root(b):
                pool.wait_ge(var_done, b + 1)
                nc.gpsimd.tensor_tensor(rstd[:], var_eps[:], minus_half[:], ALU.pow).then_inc(rstd_done, 1)

            def step(b, s, more):
                if more:
                    inverse_root(b + 1)
                for u in range(4):
                    pool.wait_ge(part1, 4 * b + u + 1)
                    nc.gpsimd.tensor_tensor(rest[:, u], qk[:, u], pieces[:, s, u, 0], ALU.subtract).then_inc(rest1, 1)
                for u in range(4):
                    pool.wait_ge(part2, 4 * b + u + 1)
                    nc.gpsimd.tensor_tensor(pieces[:, s, u, 2], rest[:, u], pieces[:, s, u, 1], ALU.subtract).then_inc(part3, 1)

            nc.gpsimd.memset(minus_half[:], -0.5).then_inc(ones_set, 1)
            pool.wait_ge(ones_set, 1)
            inverse_root(0)
            for s in range(2):
                step(s, s, True)
            with pool.Fori(1, B // 2 - 1) as i:
                for s in range(2):
                    step(2 * i + s, s, True)
            step(B - 2, 0, True)
            step(B - 1, 1, False)

        @block.tensor
        def _(pe):
            def tokens(b, s):
                for t in range(4):
                    pe.wait_ge(x_low, 4 * b + t + 1)
                    if t >= 2:
                        pe.wait_ge(h_copied, 4 * b + t - 1)
                    elif t == 0:
                        pe.wait_ge(h_copied, 4 * b)
                    rows = slice(t * P, (t + 1) * P)
                    out = tok_ps[:, t % 2, 0:C]
                    for k in range(KX):
                        nc.tensor.matmul(out, x_hi[:, k, rows], tok_hi[:, k], start=(k == 0), stop=False)
                        nc.tensor.matmul(out, x_hi[:, k, rows], tok_lo[:, k], start=False, stop=False)
                        last = nc.tensor.matmul(out, x_lo[:, k, rows], tok_hi[:, k], start=False, stop=(k == KX - 1))
                    last.then_inc(tok_done, 1)

            def transposes(b):
                pe.wait_ge(xn_done, NT * (b + 1))
                pe.wait_ge(xt_low, b)
                for c in range(NC):
                    for t in range(NT):
                        at = c * T + t * P
                        last = nc.tensor.transpose(xt_ps[:, at:at + P], xn[:, t, c * P:(c + 1) * P], ident[:])
                last.then_inc(xt_done, 1)

            def project(b):
                pe.wait_ge(xt_low, b + 1)
                pe.wait_ge(v_copied, NT * b)
                for u in range(4):
                    j, o = u // 2, slice(u % 2 * P, u % 2 * P + P)
                    for half in range(2):
                        n = 2 * u + half
                        cols = slice(half * HALF, (half + 1) * HALF)
                        if n >= 3:
                            pe.wait_ge(qk_out, 8 * b + n - 2)
                        out = ring_ps[:, n % 3, 0:HALF]
                        for c in range(NC):
                            nc.tensor.matmul(out, qkv_hi[:, j, c, o], xt_hi[:, c, cols], start=(c == 0), stop=False)
                            nc.tensor.matmul(out, qkv_hi[:, j, c, o], xt_lo[:, c, cols], start=False, stop=False)
                            last = nc.tensor.matmul(out, qkv_lo[:, j, c, o], xt_hi[:, c, cols], start=False, stop=(c == NC - 1))
                        last.then_inc(ring_qk, 1)
                for t in range(NT):
                    rows = slice(t * P, (t + 1) * P)
                    if t < 3:
                        pe.wait_ge(qk_out, 8 * b + 6 + t)
                    else:
                        pe.wait_ge(v_copied, NT * b + t - 2)
                    out = ring_ps[:, (8 + t) % 3, 0:C]
                    for c in range(NC):
                        nc.tensor.matmul(out, xt_hi[:, c, rows], qkv_hi[:, 2, c, :], start=(c == 0), stop=False)
                        nc.tensor.matmul(out, xt_hi[:, c, rows], qkv_lo[:, 2, c, :], start=False, stop=False)
                        last = nc.tensor.matmul(out, xt_lo[:, c, rows], qkv_hi[:, 2, c, :], start=False, stop=(c == NC - 1))
                    last.then_inc(ring_v, 1)

            pe.wait_ge(w_made, 7)
            tokens(0, 0)

            def step(b, s, more):
                transposes(b)
                if more:
                    tokens(b + 1, 1 - s)
                project(b)

            for s in range(2):
                step(s, s, True)
            with pe.Fori(1, B // 2 - 1) as i:
                for s in range(2):
                    step(2 * i + s, s, True)
            step(B - 2, 0, True)
            step(B - 1, 1, False)


def attention_phase(nc, a, scratch, sink):
    ctx = ExitStack()
    with ctx:
        def sb(name, shape, dt=F32):
            return ctx.enter_context(nc.sbuf_tensor(name, shape, dt))

        def sem(name):
            return ctx.enter_context(nc.semaphore(name))

        GROUPS, GH = 4, 4
        SLOTS = 2 * GROUPS
        STACK = ((0, 0), (0, 1), (0, 2), (1, 0), (1, 1), (2, 0))
        ROWS = DK * len(STACK)
        AT = {0: (0, 0), 2: (0, T), 1: (1, 0), 3: (1, 4 * P), 4: (1, 6 * P)}
        ROWS_AT = {4: (0, 0), 2: (0, T), 3: (1, 0), 1: (1, 4 * P), 0: (1, 6 * P)}
        WIDTH = (8 * P, 7 * P)
        E0 = (0, 8 * P)

        qs = sb("b_qs", [P, SLOTS, GH, T], BF16)
        ks = sb("b_ks", [P, SLOTS, GH, T], BF16)
        ex = sb("b_ex", [P, 2, GH, 15 * P])
        v_in = sb("b_v_in", [P, NT, C])
        v_pad = sb("b_v_pad", [P, 2, NT, HEADS, 2 * DK])
        h = sb("b_h", [P, 2, NT, C])
        ot = sb("b_ot", [P, 2, GROUPS, T])
        neg_max = sb("b_neg_max", [P, 2, GH, NT])
        max_rest = sb("b_max_rest", [P, GH, NT])
        max_piece = sb("b_max_piece", [P, PARTS + 1, GH, NT], BF16)
        max_rows = sb("b_max_rows", [(PARTS + 1) * GH * NT, 2, P], BF16)
        rden = sb("b_rden", [P, HEADS])
        attn = sb("b_attn", [P, C])
        at_hi = sb("b_at_hi", [P, NC, P], F32R)
        at_lo = sb("b_at_lo", [P, NC, P], F32R)
        wo = ot[:, 0, 0, 0:NC * C].rearrange("p (c o) -> p c o", c=NC)
        wo_hi = sb("b_wo_hi", [P, NC, C], F32R)
        wo_lo = sb("b_wo_lo", [P, NC, C], F32R)
        bias_o = sb("b_bias_o", [P, C])
        bias_v = sb("b_bias_v", [P, C])
        consts = sb("b_consts", [P, 3, P])
        consts_bf = sb("b_consts_bf", [P, 3, P], BF16)
        ident, ident_bf = consts[:, 0], consts_bf[:, 0]

        st_bank = ctx.enter_context(nc.psum_tensor("b_st_ps", [P, 2, 2 * BANK], F32))
        mx_bank = ctx.enter_context(nc.psum_tensor("b_mx_ps", [P, 2 * BANK], F32))
        pv_bank = ctx.enter_context(nc.psum_tensor("b_pv_ps", [P, BANK], F32))
        tail_bank = ctx.enter_context(nc.psum_tensor("b_tail_ps", [P, BANK], F32))

        const_loaded = sem("b_const_loaded")
        prep = sem("b_prep")
        ones_set = sem("b_ones_set")
        slot_loaded = [sem(f"b_slot_loaded{n}") for n in range(SLOTS)]
        neg_loaded = [sem(f"b_neg_loaded{n}") for n in range(SLOTS)]
        v_loaded = sem("b_v_loaded")
        h_loaded = [sem(f"b_h_loaded{s}") for s in range(2)]
        v_ready = sem("b_v_ready")
        h_ready = sem("b_h_ready")
        mx_done = sem("b_mx_done")
        mx_read = sem("b_mx_read")
        st_done = sem("b_st_done")
        exp_done = sem("b_exp_done")
        pv_done = sem("b_pv_done")
        ot_out = sem("b_ot_out")
        piece_done = sem("b_piece_done")
        max_turned = sem("b_max_turned")
        rows_done = sem("b_rows_done")
        rows_stored = sem("b_rows_stored")
        o_turned = sem("b_o_turned")
        rden_done = sem("b_rden_done")
        attn_done = sem("b_attn_done")
        at_turned = sem("b_at_turned")
        at_high = sem("b_at_high")
        at_low = sem("b_at_low")
        proj_done = sem("b_proj_done")
        h2_done = sem("b_h2_done")
        h2_stored = sem("b_h2_stored")

        block = ctx.enter_context(nc.Block())

        TAIL = {}
        for t in range(NT):
            TAIL[5 + 2 * t] = (0, t)
            TAIL[6 + 2 * t] = (1, t)

        def iterate(eng, step):
            step(-1, 1, False, True, False)
            step(0, 0, True, True, False)
            step(1, 1, True, True, True)
            with eng.Fori(1, B // 2 - 1) as i:
                step(2 * i, 0, True, True, True)
                step(2 * i + 1, 1, True, True, True)
            step(B - 2, 0, True, True, True)
            step(B - 1, 1, True, False, True)
            step(B, 0, False, False, True)

        def has_pv(g, cur, prev):
            return cur if g else prev

        def has_turn(g, cur, nxt):
            return nxt if g else cur

        @block.sync
        def _(sp):
            for dst, src in ((wo, a["w_o"].rearrange("(c p) o -> p c o", p=P)), (bias_o[:], a["b_o"]), (bias_v[:], a["b_v"]),
                             (consts[:], a["consts"])):
                sp.dma_start(dst, src).then_inc(const_loaded, 16)

            def load_slot(b, g, n):
                chunk, first = g // 2, g % 2 * GH
                for side, stack in ((0, qs), (1, ks)):
                    for row, pieces in enumerate(STACK):
                        src = scratch["pieces"][b].rearrange("(d h) u c t -> d u c h t", h=HPC)
                        sp.dma_start(stack[row * DK:(row + 1) * DK, n],
                                     src[:, 2 * side + chunk, pieces[side], first:first + GH]).then_inc(slot_loaded[n], 16)

            def load_v(b):
                sp.dma_start(v_in[:], scratch["v"][b]).then_inc(v_loaded, 16)

            def load_h(b, s):
                sp.dma_start(h[:, s], scratch["h"][b]).then_inc(h_loaded[s], 16)

            for n in range(SLOTS - 1):
                load_slot(n // GROUPS, n % GROUPS, n)
            load_v(0)
            for s in range(2):
                load_h(s, s)

            def step(b, s, cur, nxt, prev):
                for g in range(GROUPS):
                    nb, ng, slot = (b + 1, 3, (1 - s) * GROUPS + 3) if g == 0 else (b + 2, g - 1, s * GROUPS + g - 1)
                    if cur and (nxt if g == 0 else nxt and not (isinstance(b, int) and b + 2 >= B)):
                        sp.wait_ge(st_done, 32 * b + 8 * g)
                        load_slot(nb, ng, slot)
                    if g == 1 and cur and nxt:
                        sp.wait_ge(v_ready, b + 1)
                        load_v(b + 1)
                    if has_turn(g, cur, nxt):
                        m = 4 * b + g + 3
                        slot = s * GROUPS + 3 if g == 0 else (1 - s) * GROUPS + g - 1
                        sp.wait_ge(rows_done, m + 1)
                        sp.dma_start(scratch["neg"][slot], max_rows[0:PARTS * GH * NT, (g + 1) % 2]).then_inc(rows_stored, 16)
                        sp.wait_ge(rows_stored, 16 * (m + 1))
                        sp.dma_start(qs[ROWS:ROWS + PARTS, slot],
                                     scratch["neg"][slot].rearrange("(j h t) q -> j h (t q)", j=PARTS, h=GH))\
                          .then_inc(neg_loaded[slot], 16)
                if prev:
                    sp.wait_ge(h2_done, NT * b)
                    sp.dma_start(sink[b - 1], h[:, 1 - s]).then_inc(h2_stored, 16)
                    if nxt:
                        sp.wait_ge(h2_stored, 16 * b)
                        load_h(b + 1, 1 - s)

            iterate(sp, step)
            sp.wait_ge(h2_stored, 16 * B)

        @block.gpsimd
        def _(pool):
            nc.gpsimd.memset(ks[ROWS:P], 1.0).then_inc(ones_set, 1)
            pool.wait_ge(ones_set, 1)
            nc.gpsimd.memset(v_pad[:], 1.0).then_inc(ones_set, 1)
            pool.wait_ge(ones_set, 2)
            nc.gpsimd.memset(max_piece[:], 0.0).then_inc(ones_set, 1)
            pool.wait_ge(ones_set, 3)

            def element(b, s):
                if not (isinstance(b, int) and b < 2):
                    pool.wait_ge(pv_done, 8 * b - 8)
                pool.wait_ge(v_loaded, 16 * b + 16)
                for t in range(NT):
                    last = nc.gpsimd.tensor_tensor(v_pad[:, s, t, :, 0:DK], v_in[:, t].rearrange("p (h d) -> p h d", h=HEADS),
                                                   bias_v[:].rearrange("p (h d) -> p h d", h=HEADS), ALU.add)
                last.then_inc(v_ready, 1)
                pool.wait_ge(h_loaded[s], 8 * (b - s) + 16)
                for t in range(NT):
                    last = nc.gpsimd.tensor_tensor(h[:, s, t], h[:, s, t], bias_o[:], ALU.add)
                last.then_inc(h_ready, 1)

            pool.wait_ge(const_loaded, 64)
            element(0, 0)
            element(1, 1)
            with pool.Fori(0, B // 2 - 1) as i:
                for s in range(2):
                    element(2 * i + 2 + s, s)

        @block.scalar
        def _(act):
            def ot_copy(b, s, g, part):
                group, sg = 4 * b + g - 1, (s if g else 1 - s)
                cols = (slice(0, BANK), slice(BANK, T))[part]
                act.wait_ge(pv_done, 2 * group + part + 1)
                if (g - 1) % GROUPS == 0 and part == 0 and not (isinstance(b, int) and b < 2):
                    act.wait_ge(o_turned, NT * (b - 1))
                nc.scalar.copy(ot[:, sg, (g - 1) % GROUPS, cols], pv_bank[:, 0:cols.stop - cols.start]).then_inc(ot_out, 1)

            def step(b, s, cur, nxt, prev):
                for r in range(HEADS):
                    g, j = divmod(r, GH)
                    if j == 0 and g and has_pv(g - 1, cur, prev):
                        ot_copy(b, s, g - 1, 1)
                    if j == 0 and g == 0 and prev:
                        ot_copy(b - 1, 1 - s, 3, 1)
                    if cur:
                        for unit in range(2):
                            n = 32 * b + 2 * r + unit
                            act.wait_ge(st_done, n + 1)
                            if j == 0 and unit == 0 and not (isinstance(b, int) and 4 * b + g < 2):
                                act.wait_ge(pv_done, 2 * (4 * b + g) - 2)
                            nc.scalar.activation(ex[:, g % 2, j, E0[unit]:E0[unit] + WIDTH[unit]],
                                                 st_bank[:, unit, 0:WIDTH[unit]], ACT.Exp).then_inc(exp_done, 1)
                    if j == 1 and has_pv(g, cur, prev):
                        ot_copy(b, s, g, 0)
                    if prev and r in TAIL and TAIL[r][0] == 0:
                        n = NT * (b - 1) + TAIL[r][1]
                        act.wait_ge(at_turned, n + 1)
                        nc.scalar.copy(at_hi[:].rearrange("p c t -> p (c t)"), tail_bank[:, 0:C]).then_inc(at_high, 1)

            iterate(act, step)

        @block.vector
        def _(dve):
            dve.wait_ge(ones_set, 3)
            dve.wait_ge(const_loaded, 64)
            nc.vector.tensor_copy(consts_bf[:], consts[:]).then_inc(prep, 1)
            nc.vector.tensor_copy(wo_hi[:], wo).then_inc(prep, 1)
            dve.wait_ge(prep, 2)
            nc.vector.tensor_tensor(wo_lo[:], wo, wo_hi[:].bitcast(F32), ALU.subtract).then_inc(prep, 1)

            def row_maxima(b, r, unit):
                g, j = divmod(r, GH)
                n = 32 * b + 2 * r + unit
                dve.wait_ge(mx_done, n + 1)
                for qt, (u, col) in ROWS_AT.items():
                    if u == unit:
                        last = nc.vector.tensor_reduce(neg_max[:, g % 2, j, qt:qt + 1],
                                                       mx_bank[:, col:col + (qt + 1) * P], AX.X, ALU.max, negate=True)
                last.then_inc(mx_read, 1)

            def cut(m, g):
                if not (isinstance(m, int) and m == 0):
                    dve.wait_ge(max_turned, m)
                src = neg_max[:, (g + 1) % 2]
                dve.wait_ge(mx_read, 8 * m + 8)
                nc.vector.tensor_copy(max_piece[:, 0], src).then_inc(piece_done, 1)
                dve.wait_ge(piece_done, 4 * m + 1)
                nc.vector.tensor_tensor(max_rest[:], src, max_piece[:, 0], ALU.subtract).then_inc(piece_done, 1)
                dve.wait_ge(piece_done, 4 * m + 2)
                nc.vector.tensor_copy(max_piece[:, 1], max_rest[:]).then_inc(piece_done, 1)
                dve.wait_ge(piece_done, 4 * m + 3)
                nc.vector.tensor_tensor(max_piece[:, 2], max_rest[:], max_piece[:, 1], ALU.subtract).then_inc(piece_done, 1)

            def step(b, s, cur, nxt, prev):
                for r in range(HEADS):
                    g, j = divmod(r, GH)
                    m = 4 * b + g + 3
                    part, t = TAIL.get(r, (None, None)) if prev else (None, None)
                    if part == 0:
                        n = NT * (b - 1) + t
                        turned = tail_bank[:].rearrange("p (h d) -> p h d", d=2 * DK)
                        dve.wait_ge(o_turned, n + 1)
                        nc.vector.reciprocal(rden[:], turned[:, :, DK]).then_inc(rden_done, 1)
                        dve.wait_ge(rden_done, n + 1)
                        nc.vector.tensor_tensor(attn[:].rearrange("p (h d) -> p h d", d=DK), turned[:, :, 0:DK],
                                                rden[:].unsqueeze(2).broadcast_to([P, HEADS, DK]), ALU.mult)\
                          .then_inc(attn_done, 1)
                    if j == 0 and has_turn(g, cur, nxt):
                        cut(m, g)
                    if nxt:
                        row_maxima(b + 1, r, 0)
                    if part == 0:
                        dve.wait_ge(at_high, n + 1)
                        nc.vector.tensor_tensor(at_lo[:].rearrange("p c t -> p (c t)"), tail_bank[:, 0:C],
                                                at_hi[:].rearrange("p c t -> p (c t)").bitcast(F32), ALU.subtract)\
                          .then_inc(at_low, 1)
                    if nxt:
                        row_maxima(b + 1, r, 1)
                    if j == 2 and has_turn(g, cur, nxt):
                        if not (isinstance(m, int) and m < 2):
                            dve.wait_ge(rows_stored, 16 * (m - 1))
                        dve.wait_ge(max_turned, m + 1)
                        nc.vector.tensor_copy(max_rows[:, (g + 1) % 2], pv_bank[0:(PARTS + 1) * GH * NT, 0:P // 2].bitcast(BF16))\
                          .then_inc(rows_done, 1)
                    if part == 1:
                        n = NT * (b - 1) + t
                        dve.wait_ge(proj_done, n + 1)
                        if t == 0:
                            dve.wait_ge(h_ready, b)
                        nc.vector.tensor_tensor(h[:, 1 - s, t], tail_bank[:, 0:C], h[:, 1 - s, t], ALU.add)\
                          .then_inc(h2_done, 1)

            iterate(dve, step)

        @block.tensor
        def _(pe):
            pe.wait_ge(prep, 3)
            pe.wait_ge(ones_set, 3)

            def rows_of_scores(b, s, r, unit):
                g, j = divmod(r, GH)
                slot = s * GROUPS + g
                if j == 0 and unit == 0:
                    pe.wait_ge(slot_loaded[slot], 16 * len(STACK) * (b - s) + 32 * len(STACK))
                pe.wait_ge(mx_read, 32 * b + 2 * r + unit)
                for qt, (u, col) in ROWS_AT.items():
                    if u != unit:
                        continue
                    width = (qt + 1) * P
                    for k0 in range(0, width, BANK):
                        k1 = min(width, k0 + BANK)
                        last = nc.tensor.matmul(mx_bank[:, col + k0:col + k1], qs[0:ROWS, slot, j, qt * P:(qt + 1) * P],
                                                ks[0:ROWS, slot, j, k0:k1], start=True, stop=(k1 < width))
                    last = nc.tensor.matmul(mx_bank[:, col + width - P:col + width], ident_bf, consts_bf[:, 1],
                                            start=False, stop=True)
                last.then_inc(mx_done, 1)

            def turned_scores(b, s, r, unit):
                g, j = divmod(r, GH)
                slot = s * GROUPS + g
                n = 32 * b + 2 * r + unit
                if j == 0 and unit == 0:
                    pe.wait_ge(neg_loaded[slot], 8 * (b - s) + 16)
                if not (isinstance(n, int) and n < 2):
                    pe.wait_ge(exp_done, n - 1)
                full = ROWS + PARTS
                for kt, (u, col) in AT.items():
                    if u != unit:
                        continue
                    width = T - kt * P
                    for q0 in range(0, width, BANK):
                        q1 = min(width, q0 + BANK)
                        nc.tensor.matmul(st_bank[:, unit, col + q0:col + q1], ks[0:full, slot, j, kt * P:(kt + 1) * P],
                                         qs[0:full, slot, j, kt * P + q0:kt * P + q1], start=True, stop=(q0 > 0))
                        if q0 == 0:
                            last = nc.tensor.matmul(st_bank[:, unit, col:col + P], ident_bf, consts_bf[:, 2],
                                                    start=False, stop=True)
                last.then_inc(st_done, 1)

            def weighted_values(b, s, g, j):
                group, sg, vg = 4 * b + g - 1, (g - 1) % 2, (s if g else 1 - s)
                heads = (g - 1) % GROUPS * GH
                if j == 0:
                    pe.wait_ge(v_ready, b + 1 if g else b)
                    pe.wait_ge(exp_done, 8 * group + 8)
                    pe.wait_ge(ot_out, 2 * group)
                tiles = {0: (0,), 1: (1, 2, 3), 3: (0, 1, 2, 3, 4)}[j]
                for kt in tiles:
                    unit, col = AT[kt]
                    col += E0[unit]
                    if j < 3:
                        q0, q1 = kt * P, BANK
                    else:
                        q0, q1 = BANK, T
                    base = 0 if j < 3 else BANK
                    for n in range(GH):
                        last = nc.tensor.matmul(pv_bank[2 * DK * n:2 * DK * (n + 1), q0 - base:q1 - base],
                                                v_pad[:, vg, kt, heads + n],
                                                ex[:, sg, n, col + q0 - kt * P:col + q1 - kt * P],
                                                start=(kt == 0), stop=(kt == tiles[-1] and j > 0))
                if j:
                    last.then_inc(pv_done, 1)

            def step(b, s, cur, nxt, prev):
                for r in range(HEADS):
                    g, j = divmod(r, GH)
                    m = 4 * b + g + 3
                    part, t = TAIL.get(r, (None, None)) if prev else (None, None)
                    n = NT * (b - 1) + t if part is not None else None
                    if part == 0:
                        pe.wait_ge(ot_out, 8 * b)
                        pe.wait_ge(h2_done, n)
                        for u in range(GROUPS):
                            last = nc.tensor.transpose(tail_bank[:, u * P:(u + 1) * P],
                                                       ot[:, 1 - s, u, t * P:(t + 1) * P], ident)
                        last.then_inc(o_turned, 1)
                    if nxt:
                        rows_of_scores(b + 1, 1 - s, r, 0)
                    if cur:
                        turned_scores(b, s, r, 0)
                    if j < 2 and has_pv(g, cur, prev):
                        weighted_values(b, s, g, j)
                    if part == 0:
                        pe.wait_ge(attn_done, n + 1)
                        for c in range(NC):
                            last = nc.tensor.transpose(tail_bank[:, c * P:(c + 1) * P], attn[:, c * P:(c + 1) * P], ident)
                        last.then_inc(at_turned, 1)
                    if nxt:
                        rows_of_scores(b + 1, 1 - s, r, 1)
                    if cur:
                        turned_scores(b, s, r, 1)
                    if j == 2 and has_turn(g, cur, nxt):
                        pe.wait_ge(piece_done, 4 * m + 4)
                        if has_pv(g, cur, prev):
                            pe.wait_ge(ot_out, 2 * (4 * b + g) - 1)
                        nc.tensor.transpose(pv_bank[0:(PARTS + 1) * GH * NT, 0:P // 2].bitcast(BF16),
                                            max_piece[:].rearrange("p j h t -> p (j h t)"), ident_bf).then_inc(max_turned, 1)
                    if j == 3 and has_pv(g, cur, prev):
                        if has_turn(g, cur, nxt):
                            pe.wait_ge(rows_done, m + 1)
                        else:
                            pe.wait_ge(ot_out, 2 * (4 * b + g) - 1)
                        weighted_values(b, s, g, j)
                    if part == 1:
                        pe.wait_ge(at_low, n + 1)
                        for c in range(NC):
                            nc.tensor.matmul(tail_bank[:, 0:C], at_hi[:, c], wo_hi[:, c], start=(c == 0), stop=False)
                            nc.tensor.matmul(tail_bank[:, 0:C], at_hi[:, c], wo_lo[:, c], start=False, stop=False)
                            last = nc.tensor.matmul(tail_bank[:, 0:C], at_lo[:, c], wo_hi[:, c], start=False, stop=(c == NC - 1))
                        last.then_inc(proj_done, 1)

            iterate(pe, step)


def expert_phase(nc, a, scratch, out):
    E, H = 16, 128
    W3 = 3 * H
    SCALE = 1.0 / float(H) ** 0.5
    LOW = -1e30
    OG = E // 2
    ctx = ExitStack()
    with ctx:
        def sb(name, shape, dt=F32):
            return ctx.enter_context(nc.sbuf_tensor(name, shape, dt))

        def sem(name):
            return ctx.enter_context(nc.semaphore(name))

        p_hi = sb("c_p_hi", [P, NC, E, W3], F32R)
        p_lo = sb("c_p_lo", [P, NC, E, W3], F32R)
        o_hi = sb("c_o_hi", [P, E, C], F32R)
        o_lo = sb("c_o_lo", [P, E, C], F32R)
        ident = sb("c_ident", [P, P])
        ones = sb("c_ones", [P, P])
        sim = sb("c_sim", [P, NC, E])
        sim_sq = sb("c_sim_sq", [P, NC, E])
        sim_ss = sb("c_sim_ss", [P, E])
        sim_rn = sb("c_sim_rn", [P, E])
        sim_n = sb("c_sim_n", [P, NC, E])
        sim_hi = sb("c_sim_hi", [P, NC, E], F32R)
        sim_lo = sb("c_sim_lo", [P, NC, E], F32R)
        gates = sb("c_gates", [P, E])
        gate_e = sb("c_gate_e", [P, E])
        gate_1 = sb("c_gate_1", [P, E])
        gate_s = sb("c_gate_s", [P, E])
        first = sb("c_first", [P, E])
        minus_half = sb("c_minus_half", [P, E])

        h_ln = sb("c_h_ln", [P, NT, C])
        h_res = sb("c_h_res", [P, NT, C])
        stats = sb("c_stats", [P, NT, 6])
        sums = sb("c_sums", [P, NT, 2])
        diff = sb("c_diff", [P, NT, 1])
        mean = sb("c_mean", [P, NT, 1])
        spread = sb("c_spread", [P, NT, 1])
        var = sb("c_var", [P, NT, 1])
        var_eps = sb("c_var_eps", [P, NT, 1])
        rstd = sb("c_rstd", [P, NT, 1])
        xf = sb("c_xf", [P, NT, C])
        sq = sb("c_sq", [P, C])
        ssq = sb("c_ssq", [P, NT, 1])
        ssq_c = sb("c_ssq_c", [P, NT, 1])
        rnorm = sb("c_rnorm", [P, NT, 1])
        xt_hi = sb("c_xt_hi", [P, 2, NC, T], F32R)
        xt_lo = sb("c_xt_lo", [P, 2, NC, T], F32R)
        raw = sb("c_raw", [P, NT, E])
        logit = sb("c_logit", [P, NT, E])
        gated = sb("c_gated", [P, NT, E])
        hard = sb("c_hard", [P, NT, E])
        active = sb("c_active", [P, NT, 1])
        top = sb("c_top", [P, NT, 1])
        cand = sb("c_cand", [P, NT, E])
        rank = sb("c_rank", [P, NT, 1])
        hot1 = sb("c_hot1", [P, NT, E])
        hot2 = sb("c_hot2", [P, NT, E])
        left = sb("c_left", [P, NT, E])
        mask = sb("c_mask", [P, NT, E])
        gexp = sb("c_gexp", [P, NT, E])
        wsum = sb("c_wsum", [P, NT, 1])
        w = sb("c_w", [P, 2, NT, E])
        wn = sb("c_wn", [P, NT, E])
        qkv = sb("c_qkv", [P, 2, NT, W3])
        qkv_odd = sb("c_qkv_odd", [P, 2, W3])
        qk_t = sb("c_qk_t", [P, 2, T])
        neg_max = sb("c_neg_max", [P, NT])
        bias = sb("c_bias", [P, NT])
        denom = sb("c_denom", [P, NT, 1])
        rden = sb("c_rden", [P, NT, 1])
        ex = sb("c_ex", [P, 2, T])
        ex_t = sb("c_ex_t", [P, NT, T])
        ot_hi = sb("c_ot_hi", [P, T], F32R)
        ot_lo = sb("c_ot_lo", [P, T], F32R)
        y_odd = sb("c_y_odd", [P, 2, C])
        STAGES, STAGE = 3, NC * W3 + C
        flat = ex_t[:].rearrange("p t k -> p (t k)")
        stage = [flat[:, n * STAGE:(n + 1) * STAGE] for n in range(STAGES)]
        stage_p = [x[:, 0:NC * W3].rearrange("p (c j) -> p c j", c=NC) for x in stage]
        stage_o = [x[:, NC * W3:STAGE] for x in stage]

        q_bank = ctx.enter_context(nc.psum_tensor("c_q_ps", [P, 3, BANK], F32))
        x_bank = ctx.enter_context(nc.psum_tensor("c_x_ps", [P, 2, BANK], F32))
        y_bank = ctx.enter_context(nc.psum_tensor("c_y_ps", [P, 2, BANK], F32))
        x_flat = x_bank[:].rearrange("p a c -> p (a c)")
        y_flat = y_bank[:].rearrange("p a c -> p (a c)")

        const_loaded = sem("c_const_loaded")
        set_up = sem("c_set_up")
        pool_up = sem("c_pool_up")
        gate_exp = sem("c_gate_exp")
        sim_sum = sem("c_sim_sum")
        stage_loaded = [sem(f"c_stage_loaded{n}") for n in range(STAGES)]
        w_high = sem("c_w_high")
        w_low = sem("c_w_low")
        hl_loaded = sem("c_hl_loaded")
        hr_loaded = sem("c_hr_loaded")
        stat_done = sem("c_stat_done")
        var_step = sem("c_var_step")
        var_done = sem("c_var_done")
        rstd_done = sem("c_rstd_done")
        xf_done = sem("c_xf_done")
        ssq_done = sem("c_ssq_done")
        ssq_ready = sem("c_ssq_ready")
        rnorm_done = sem("c_rnorm_done")
        xf_turned = sem("c_xf_turned")
        xf_high = sem("c_xf_high")
        xf_low = sem("c_xf_low")
        logit_done = sem("c_logit_done")
        route = sem("c_route")
        gexp_done = sem("c_gexp_done")
        w_done = sem("c_w_done")
        q_done = sem("c_q_done")
        q_acc = sem("c_q_acc")
        qkv_done = sem("c_qkv_done")
        qk_turned = sem("c_qk_turned")
        qk_out = sem("c_qk_out")
        s_done = sem("c_s_done")
        s_max = sem("c_s_max")
        bias_done = sem("c_bias_done")
        ex_done = sem("c_ex_done")
        ex_turned = sem("c_ex_turned")
        ex_out = sem("c_ex_out")
        rden_done = sem("c_rden_done")
        wn_done = sem("c_wn_done")
        ot_done = sem("c_ot_done")
        ot_high = sem("c_ot_high")
        ot_low = sem("c_ot_low")
        y_done = sem("c_y_done")
        y_acc = sem("c_y_acc")
        y_out = sem("c_y_out")
        y_stored = sem("c_y_stored")
        ROUTE, ROUTE_PARTS = 14, 4
        route_top = sem("c_route_top")
        mask_step = sem("c_mask_step")
        w_step = sem("c_w_step")

        block = ctx.enter_context(nc.Block())

        PIECES = [[] for _ in range(NT * E)]
        for n in range(2):
            PIECES[3 + 4 * n].append(("turn_qk", n))
        for t in range(NT):
            PIECES[15 + 4 * t].append(("turn_ex", t))
            PIECES[11 + 4 * t].append(("scores", t))
            PIECES[13 + 4 * t].append(("stats", t))
            PIECES[34 + 2 * t].append(("norm", t))
        for n in range(2):
            PIECES[34 + 4 * n].append(("values", n))
        for n in range(NT * OG):
            PIECES[NT * OG + n].append(("output", n))
        for c in range(NC):
            PIECES[48 + 4 * c].append(("turn_xf", c))
        for n in range(ROUTE_PARTS):
            PIECES[56 + 4 * n].append(("route", n))
        NEXT = ("stats", "norm", "turn_xf", "route")

        def iterate(eng, expert, piece):
            def run(b, s, attend, project, ahead):
                for p, pieces in enumerate(PIECES):
                    if project:
                        expert(b + 1, 1 - s, *divmod(p, E))
                    for kind, n in pieces:
                        if kind in NEXT:
                            if ahead:
                                piece(kind, b + 2, s, n)
                        elif attend:
                            piece(kind, b, s, n)

            run(-2, 0, False, False, True)
            run(-1, 1, False, True, True)
            run(0, 0, True, True, True)
            run(1, 1, True, True, True)
            with eng.Fori(1, B // 2 - 1) as i:
                run(2 * i, 0, True, True, True)
                run(2 * i + 1, 1, True, True, True)
            run(B - 2, 0, True, True, False)
            run(B - 1, 1, True, False, False)

        @block.sync
        def _(sp):
            for dst, src in ((sim[:], a["sim"].rearrange("(c p) e -> p c e", p=P)), (gates[:], a["gates"]),
                             (ident[:], a["ident"]), (first[:], a["first"])):
                sp.dma_start(dst, src).then_inc(const_loaded, 16)
            sp.dma_start(h_ln[:], scratch["h2"][0]).then_inc(hl_loaded, 16)
            for e in range(E):
                n = e % STAGES
                if e >= STAGES:
                    sp.wait_ge(w_low, e - STAGES + 1)
                sp.dma_start(stage[n], a["w_exp"][e]).then_inc(stage_loaded[n], 16)
            sp.dma_start(h_res[:], scratch["h2"][0]).then_inc(hr_loaded, 16)

            def step(b, load_ln, load_res):
                if load_ln:
                    sp.wait_ge(ssq_done, NT * (b + 3))
                    sp.wait_ge(xf_done, NT * (b + 3))
                    sp.dma_start(h_ln[:], scratch["h2"][b + 3]).then_inc(hl_loaded, 16)
                if not (isinstance(b, int) and b < 0):
                    sp.wait_ge(y_out, NT * (b + 1))
                    sp.dma_start(out[b].rearrange("(t p) c -> p t c", p=P), h_res[:]).then_inc(y_stored, 16)
                    if load_res:
                        sp.wait_ge(y_stored, 16 * (b + 1))
                        sp.dma_start(h_res[:], scratch["h2"][b + 1]).then_inc(hr_loaded, 16)

            step(-2, True, False)
            step(-1, True, False)
            with sp.Fori(0, B - 3) as b:
                step(b, True, True)
            for b in range(B - 3, B):
                step(b, False, b + 1 < B)
            sp.wait_ge(y_stored, 16 * B)

        @block.gpsimd
        def _(pool):
            nc.gpsimd.memset(minus_half[:], -0.5).then_inc(pool_up, 1)
            pool.wait_ge(pool_up, 1)
            nc.gpsimd.memset(ones[:], 1.0).then_inc(pool_up, 1)
            pool.wait_ge(set_up, 2)
            nc.gpsimd.tensor_tensor(sim_rn[:], sim_ss[:], minus_half[:], ALU.pow).then_inc(pool_up, 1)

            def expert(b, s, t, e):
                if e == E - 1:
                    pool.wait_ge(q_acc, NT * E * b + E * (t + 1))
                    nc.gpsimd.tensor_tensor(qkv[:, s, t], qkv[:, s, t], qkv_odd[:, t % 2], ALU.add).then_inc(qkv_done, 1)

            def piece(kind, b, s, n):
                if kind == "stats" and n == NT - 1:
                    pool.wait_ge(var_done, b + 1)
                    nc.gpsimd.tensor_tensor(rstd[:], var_eps[:], minus_half[:, 0:NT].unsqueeze(2), ALU.pow).then_inc(rstd_done, 1)
                if kind == "norm" and n == NT - 1:
                    pool.wait_ge(ssq_ready, b + 1)
                    nc.gpsimd.tensor_tensor(rnorm[:], ssq_c[:], minus_half[:, 0:NT].unsqueeze(2), ALU.pow).then_inc(rnorm_done, 1)
                if kind == "output" and n % OG == OG - 1:
                    t = n // OG
                    pool.wait_ge(y_acc, NT * E * b + E * (t + 1))
                    nc.gpsimd.tensor_tensor(h_res[:, t], h_res[:, t], y_odd[:, t % 2], ALU.add).then_inc(y_out, 1)

            iterate(pool, expert, piece)

        @block.scalar
        def _(act):
            act.wait_ge(const_loaded, 64)
            nc.scalar.activation(gate_e[:], gates[:], ACT.Exp, scale=-1.0).then_inc(gate_exp, 1)

            def expert(b, s, t, e):
                if isinstance(b, int) and b == 0 and t == 0:
                    act.wait_ge(stage_loaded[e % STAGES], 16 * (e // STAGES + 1))
                    nc.scalar.copy(p_hi[:, :, e], stage_p[e % STAGES])
                    nc.scalar.copy(o_hi[:, e], stage_o[e % STAGES]).then_inc(w_high, 1)

            def piece(kind, b, s, n):
                if kind == "turn_qk":
                    act.wait_ge(qk_turned, 2 * b + n + 1)
                    nc.scalar.copy(qk_t[:, n], x_flat[:, 0:T]).then_inc(qk_out, 1)
                if kind == "scores":
                    act.wait_ge(bias_done, NT * b + n + 1)
                    act.wait_ge(ex_turned, NT * b + n - 1 if n else NT * b)
                    nc.scalar.activation(ex[:, n % 2].rearrange("p (a k) -> p a k", a=2), x_bank[:, :, 0:HALF], ACT.Exp,
                                         bias=bias[:, n:n + 1], scale=SCALE, accum_out=denom[:, n]).then_inc(ex_done, 1)
                if kind == "turn_ex":
                    act.wait_ge(ex_turned, NT * b + n + 1)
                    nc.scalar.copy(ex_t[:, :, n * P:(n + 1) * P],
                                   y_flat[:, 0:T].rearrange("p (t q) -> p t q", t=NT)).then_inc(ex_out, 1)
                if kind == "values":
                    act.wait_ge(ot_done, 2 * b + n + 1)
                    nc.scalar.copy(ot_hi[:, n * HALF:(n + 1) * HALF], y_bank[:, n, 0:HALF]).then_inc(ot_high, 1)
                if kind == "turn_xf":
                    act.wait_ge(xf_turned, NC * b + n + 1)
                    nc.scalar.copy(xt_hi[:, s, n], x_flat[:, 0:T]).then_inc(xf_high, 1)
                if kind == "route" and n == 0:
                    act.wait_ge(route, ROUTE * b + 3)
                    nc.scalar.activation(gexp[:], gated[:], ACT.Exp).then_inc(gexp_done, 1)

            iterate(act, expert, piece)

        @block.vector
        def _(dve):
            dve.wait_ge(const_loaded, 64)
            nc.vector.tensor_tensor(sim_sq[:], sim[:], sim[:], ALU.mult).then_inc(set_up, 1)
            dve.wait_ge(sim_sum, 1)
            nc.vector.tensor_scalar(sim_ss[:], x_bank[:, 0, 0:E], 1e-24, None, ALU.max).then_inc(set_up, 1)
            dve.wait_ge(pool_up, 3)
            nc.vector.tensor_tensor(sim_n[:], sim[:], sim_rn[:].unsqueeze(1).broadcast_to([P, NC, E]), ALU.mult)\
              .then_inc(set_up, 1)
            dve.wait_ge(gate_exp, 1)
            nc.vector.tensor_scalar(gate_1[:], gate_e[:], 1.0, None, ALU.add).then_inc(set_up, 1)
            dve.wait_ge(set_up, 4)
            nc.vector.reciprocal(gate_s[:], gate_1[:]).then_inc(set_up, 1)
            nc.vector.tensor_copy(sim_hi[:], sim_n[:]).then_inc(set_up, 1)
            dve.wait_ge(set_up, 6)
            nc.vector.tensor_tensor(sim_lo[:], sim_n[:], sim_hi[:].bitcast(F32), ALU.subtract).then_inc(set_up, 1)

            def low_halves(e):
                dve.wait_ge(w_high, e + 1)
                nc.vector.tensor_tensor(p_lo[:, :, e], stage_p[e % STAGES], p_hi[:, :, e].bitcast(F32), ALU.subtract)
                nc.vector.tensor_tensor(o_lo[:, e], stage_o[e % STAGES], o_hi[:, e].bitcast(F32), ALU.subtract)\
                  .then_inc(w_low, 1)

            def expert(b, s, t, e):
                n = NT * E * b + E * t + e
                acc = qkv_odd[:, t % 2] if e % 2 else qkv[:, s, t]
                if isinstance(b, int) and b == 0 and t == 0:
                    for ahead in range(e + STAGES - 1 if e else 0, min(e + STAGES, E)):
                        low_halves(ahead)
                if e == 0:
                    if t == 0:
                        dve.wait_ge(w_done, b + 1)
                        dve.wait_ge(qkv_done, NT * b)
                    elif t >= 2:
                        dve.wait_ge(qkv_done, NT * b + t - 1)
                dve.wait_ge(q_done, n + 1)
                src = q_bank[:, (E * t + e) % 3, 0:W3]
                if e < 2:
                    nc.vector.tensor_scalar(acc, src, w[:, s, t, e:e + 1], None, ALU.mult).then_inc(q_acc, 1)
                else:
                    dve.wait_ge(q_acc, n - 1)
                    nc.vector.scalar_tensor_tensor(out=acc, in0=src, scalar=w[:, s, t, e:e + 1], in1=acc,
                                                   op0=ALU.mult, op1=ALU.add).then_inc(q_acc, 1)

            def router(b, s, part):
                def after(k):
                    dve.wait_ge(route, ROUTE * b + k)

                def wide(x):
                    return x[:].broadcast_to([P, NT, E])

                if part == 0:
                    dve.wait_ge(logit_done, b + 1)
                    dve.wait_ge(rnorm_done, b + 1)
                    nc.vector.tensor_tensor(raw[:], x_flat[:, 0:NT * E].rearrange("p (t e) -> p t e", e=E),
                                            wide(rnorm), ALU.mult).then_inc(route, 1)
                    after(1)
                    nc.vector.tensor_tensor(logit[:], raw[:], gate_s[:].unsqueeze(1).broadcast_to([P, NT, E]),
                                            ALU.subtract).then_inc(route, 1)
                    after(2)
                    nc.vector.tensor_scalar(gated[:], logit[:], 0.0, None, ALU.max).then_inc(route, 1)
                    nc.vector.tensor_scalar(hard[:], logit[:], 0.0, None, ALU.is_gt).then_inc(route, 1)
                    nc.vector.tensor_reduce(top[:], logit[:], AX.X, ALU.max).then_inc(route, 1)
                    after(5)
                    nc.vector.tensor_reduce(active[:], hard[:], AX.X, ALU.max).then_inc(mask_step, 1)
                if part == 1 or part == 2:
                    best, src, k = ((hot1, logit, 5), (hot2, left, 10))[part - 1]
                    nc.vector.tensor_tensor(best[:], src[:], wide(top), ALU.is_equal).then_inc(route, 1)
                    after(k + 1)
                    nc.vector.tensor_tensor(cand[:], best[:], first[:].unsqueeze(1).broadcast_to([P, NT, E]),
                                            ALU.mult).then_inc(route, 1)
                    after(k + 2)
                    nc.vector.tensor_reduce(rank[:], cand[:], AX.X, ALU.max).then_inc(route, 1)
                    after(k + 3)
                    nc.vector.tensor_tensor(best[:], cand[:], wide(rank), ALU.is_equal).then_inc(route, 1)
                    after(k + 4)
                if part == 1:
                    nc.vector.scalar_tensor_tensor(out=left[:], in0=hot1[:], scalar=LOW, in1=logit[:],
                                                   op0=ALU.mult, op1=ALU.add).then_inc(route, 1)
                    after(10)
                    nc.vector.tensor_reduce(top[:], left[:], AX.X, ALU.max).then_inc(route_top, 1)
                    dve.wait_ge(route_top, b + 1)
                if part < 3:
                    return
                nc.vector.tensor_tensor(cand[:], hot1[:], hot2[:], ALU.add).then_inc(mask_step, 1)
                dve.wait_ge(mask_step, 5 * b + 2)
                nc.vector.tensor_tensor(left[:], cand[:], wide(active), ALU.is_gt).then_inc(mask_step, 1)
                dve.wait_ge(mask_step, 5 * b + 3)
                nc.vector.tensor_tensor(mask[:], hard[:], left[:], ALU.max).then_inc(mask_step, 1)
                dve.wait_ge(mask_step, 5 * b + 4)
                dve.wait_ge(gexp_done, b + 1)
                nc.vector.tensor_tensor(cand[:], gexp[:], mask[:], ALU.mult).then_inc(mask_step, 1)
                dve.wait_ge(mask_step, 5 * b + 5)
                nc.vector.tensor_reduce(wsum[:], cand[:], AX.X, ALU.add).then_inc(w_step, 1)
                dve.wait_ge(w_step, 2 * b + 1)
                nc.vector.reciprocal(rank[:], wsum[:]).then_inc(w_step, 1)
                dve.wait_ge(w_step, 2 * b + 2)
                nc.vector.tensor_tensor(w[:, s], cand[:], wide(rank), ALU.mult).then_inc(w_done, 1)

            def piece(kind, b, s, n):
                if kind == "stats":
                    dve.wait_ge(hl_loaded, 16 * (b + 1))
                    nc.vector.bn_stats(stats[:, n], h_ln[:, n]).then_inc(stat_done, 1)
                if kind == "stats" and n == NT - 1:
                    dve.wait_ge(stat_done, NT * (b + 1))
                    even, odd = stats[:, :, 0:3], stats[:, :, 3:6]
                    nc.vector.tensor_tensor(sums[:], even[:, :, 1:3], odd[:, :, 1:3], ALU.add).then_inc(var_step, 1)
                    nc.vector.tensor_tensor(diff[:], even[:, :, 1:2], odd[:, :, 1:2], ALU.subtract).then_inc(var_step, 1)
                    dve.wait_ge(var_step, 5 * b + 2)
                    nc.vector.tensor_scalar(mean[:], sums[:, :, 0:1], 0.5, None, ALU.mult).then_inc(var_step, 1)
                    nc.vector.scalar_tensor_tensor(out=spread[:], in0=diff[:], scalar=0.25, in1=diff[:],
                                                   op0=ALU.mult, op1=ALU.mult).then_inc(var_step, 1)
                    dve.wait_ge(var_step, 5 * b + 4)
                    nc.vector.scalar_tensor_tensor(out=var[:], in0=sums[:, :, 1:2], scalar=1.0 / C, in1=spread[:],
                                                   op0=ALU.mult, op1=ALU.add).then_inc(var_step, 1)
                    dve.wait_ge(var_step, 5 * b + 5)
                    nc.vector.tensor_scalar(var_eps[:], var[:], EPS, None, ALU.add).then_inc(var_done, 1)
                if kind == "norm":
                    if n == 0:
                        dve.wait_ge(rstd_done, b + 1)
                    nc.vector.tensor_scalar(xf[:, n], h_ln[:, n], mean[:, n, 0:1], rstd[:, n, 0:1],
                                            ALU.subtract, ALU.mult).then_inc(xf_done, 1)
                    dve.wait_ge(xf_done, NT * b + n + 1)
                    dve.wait_ge(ssq_done, NT * b + n)
                    nc.vector.tensor_tensor_reduce(out=sq[:], in0=xf[:, n], in1=xf[:, n], scale=1.0, scalar=0.0,
                                                   op0=ALU.mult, op1=ALU.add, accum_out=ssq[:, n]).then_inc(ssq_done, 1)
                if kind == "norm" and n == NT - 1:
                    dve.wait_ge(ssq_done, NT * (b + 1))
                    nc.vector.tensor_scalar(ssq_c[:], ssq[:], 1e-24, None, ALU.max).then_inc(ssq_ready, 1)
                if kind == "turn_xf":
                    dve.wait_ge(xf_high, NC * b + n + 1)
                    nc.vector.tensor_tensor(xt_lo[:, s, n], x_flat[:, 0:T], xt_hi[:, s, n].bitcast(F32),
                                            ALU.subtract).then_inc(xf_low, 1)
                if kind == "route":
                    router(b, s, n)
                if kind == "scores":
                    dve.wait_ge(s_done, NT * b + n + 1)
                    nc.vector.tensor_reduce(neg_max[:, n:n + 1], x_bank[:, :, 0:HALF], AX.XY, ALU.max, negate=True)\
                      .then_inc(s_max, 1)
                    dve.wait_ge(s_max, NT * b + n + 1)
                    nc.vector.tensor_scalar(bias[:, n:n + 1], neg_max[:, n:n + 1], SCALE, None, ALU.mult).then_inc(bias_done, 1)
                if kind == "values":
                    if n == 0:
                        dve.wait_ge(ex_done, NT * (b + 1))
                        nc.vector.reciprocal(rden[:], denom[:]).then_inc(rden_done, 1)
                        dve.wait_ge(rden_done, b + 1)
                        nc.vector.tensor_tensor(wn[:], w[:, s], rden[:].broadcast_to([P, NT, E]), ALU.mult)\
                          .then_inc(wn_done, 1)
                    dve.wait_ge(ot_high, 2 * b + n + 1)
                    cols = slice(n * HALF, (n + 1) * HALF)
                    nc.vector.tensor_tensor(ot_lo[:, cols], y_bank[:, n, 0:HALF], ot_hi[:, cols].bitcast(F32),
                                            ALU.subtract).then_inc(ot_low, 1)
                if kind == "output":
                    t = n // OG
                    if n == 0:
                        dve.wait_ge(wn_done, b + 1)
                        dve.wait_ge(hr_loaded, 16 * (b + 1))
                        dve.wait_ge(y_out, NT * b)
                    elif n % OG == 0 and t >= 2:
                        dve.wait_ge(y_out, NT * b + t - 1)
                    pair = n % OG
                    for e in range(2 * pair, 2 * pair + 2):
                        k = NT * E * b + E * t + e
                        src = y_bank[:, e // 2 % 2, e % 2 * C:(e % 2 + 1) * C]
                        acc = y_odd[:, t % 2] if e % 2 else h_res[:, t]
                        if e % 2 == 0:
                            dve.wait_ge(y_done, NT * OG * b + OG * t + e // 2 + 1)
                        if e == 1:
                            nc.vector.tensor_scalar(acc, src, wn[:, t, e:e + 1], None, ALU.mult).then_inc(y_acc, 1)
                        else:
                            if e > 1:
                                dve.wait_ge(y_acc, k - 1)
                            nc.vector.scalar_tensor_tensor(out=acc, in0=src, scalar=wn[:, t, e:e + 1], in1=acc,
                                                           op0=ALU.mult, op1=ALU.add).then_inc(y_acc, 1)

            iterate(dve, expert, piece)

        @block.tensor
        def _(pe):
            pe.wait_ge(set_up, 1)
            pe.wait_ge(pool_up, 2)
            for c in range(NC):
                last = nc.tensor.matmul(x_bank[:, 0, 0:E], ones[:], sim_sq[:, c], start=(c == 0), stop=(c == NC - 1))
            last.then_inc(sim_sum, 1)
            pe.wait_ge(set_up, 7)

            def expert(b, s, t, e):
                rows = slice(t * P, (t + 1) * P)
                n = E * t + e
                if n == 0:
                    pe.wait_ge(xf_low, NC * (b + 1))
                    pe.wait_ge(q_acc, NT * E * b)
                if isinstance(b, int) and b == 0 and t == 0:
                    pe.wait_ge(w_low, e + 1)
                if n >= 3:
                    pe.wait_ge(q_acc, NT * E * b + n - 2)
                dst = q_bank[:, n % 3, 0:W3]
                for c in range(NC):
                    nc.tensor.matmul(dst, xt_hi[:, s, c, rows], p_hi[:, c, e], start=(c == 0), stop=False)
                    nc.tensor.matmul(dst, xt_hi[:, s, c, rows], p_lo[:, c, e], start=False, stop=False)
                    last = nc.tensor.matmul(dst, xt_lo[:, s, c, rows], p_hi[:, c, e], start=False, stop=(c == NC - 1))
                last.then_inc(q_done, 1)

            def piece(kind, b, s, n):
                if kind == "turn_qk":
                    if n == 0:
                        pe.wait_ge(qkv_done, NT * (b + 1))
                        pe.wait_ge(w_done, b + 1)
                    else:
                        pe.wait_ge(qk_out, 2 * b + 1)
                    for t in range(NT):
                        last = nc.tensor.transpose(x_flat[:, t * P:(t + 1) * P], qkv[:, s, t, n * H:(n + 1) * H], ident[:])
                    last.then_inc(qk_turned, 1)
                if kind == "scores":
                    pe.wait_ge(qk_out, 2 * (b + 1))
                    pe.wait_ge(ex_done, NT * b + n)
                    for half in range(2):
                        last = nc.tensor.matmul(x_bank[:, half, 0:HALF], qk_t[:, 0, n * P:(n + 1) * P],
                                                qk_t[:, 1, half * HALF:(half + 1) * HALF], start=True, stop=True)
                    last.then_inc(s_done, 1)
                if kind == "turn_ex":
                    if n == 0:
                        pe.wait_ge(y_acc, NT * E * b)
                    pe.wait_ge(ex_out, NT * b + n)
                    pe.wait_ge(ex_done, NT * b + n + 1)
                    for t in range(NT):
                        last = nc.tensor.transpose(y_flat[:, t * P:(t + 1) * P], ex[:, n % 2, t * P:(t + 1) * P], ident[:])
                    last.then_inc(ex_turned, 1)
                if kind == "values":
                    pe.wait_ge(ex_out, NT * (b + 1))
                    for t in range(NT):
                        last = nc.tensor.matmul(y_bank[:, n, 0:HALF], qkv[:, s, t, 2 * H:3 * H],
                                                ex_t[:, t, n * HALF:(n + 1) * HALF], start=(t == 0), stop=(t == NT - 1))
                    last.then_inc(ot_done, 1)
                if kind == "output":
                    t, pair = divmod(n, OG)
                    rows = slice(t * P, (t + 1) * P)
                    if n == 0:
                        pe.wait_ge(ot_low, 2 * (b + 1))
                    if n >= 2:
                        pe.wait_ge(y_acc, NT * E * b + 2 * (n - 1))
                    dst = y_bank[:, n % 2]
                    hi = o_hi[:, 2 * pair:2 * pair + 2].rearrange("p e c -> p (e c)")
                    lo = o_lo[:, 2 * pair:2 * pair + 2].rearrange("p e c -> p (e c)")
                    nc.tensor.matmul(dst, ot_hi[:, rows], hi, start=True, stop=False)
                    nc.tensor.matmul(dst, ot_hi[:, rows], lo, start=False, stop=False)
                    nc.tensor.matmul(dst, ot_lo[:, rows], hi, start=False, stop=True).then_inc(y_done, 1)
                if kind == "turn_xf":
                    pe.wait_ge(xf_done, NT * (b + 1))
                    pe.wait_ge(xf_low, NC * b + n)
                    if not (isinstance(b, int) and b < 2):
                        pe.wait_ge(ex_done, NT * (b - 1))
                    for t in range(NT):
                        last = nc.tensor.transpose(x_flat[:, t * P:(t + 1) * P], xf[:, t, n * P:(n + 1) * P], ident[:])
                    last.then_inc(xf_turned, 1)
                if kind == "route" and n == 0:
                    pe.wait_ge(xf_low, NC * (b + 1))
                    for t in range(NT):
                        rows, dst = slice(t * P, (t + 1) * P), x_flat[:, t * E:(t + 1) * E]
                        for c in range(NC):
                            nc.tensor.matmul(dst, xt_hi[:, s, c, rows], sim_hi[:, c], start=(c == 0), stop=False)
                            nc.tensor.matmul(dst, xt_hi[:, s, c, rows], sim_lo[:, c], start=False, stop=False)
                            last = nc.tensor.matmul(dst, xt_lo[:, s, c, rows], sim_hi[:, c], start=False, stop=(c == NC - 1))
                    last.then_inc(logit_done, 1)

            iterate(pe, expert, piece)


def layout(inputs):
    import numpy as np

    def get(name):
        return np.asarray(inputs[name])

    def cont(v):
        return np.ascontiguousarray(v)

    order = np.arange(C).reshape(NC, HPC, DK).transpose(0, 2, 1).reshape(-1)
    w_qkv = np.stack([get("L0_attn_Wq").T[:, order], get("L0_attn_Wk").T[:, order], get("L0_attn_Wv").T])
    b_qk = np.stack([get("L0_attn_bq")[order].reshape(NC, P).T, get("L0_attn_bk")[order].reshape(NC, P).T], axis=1)
    p_qkv = np.concatenate([get(f"L0_ffn_{n}_proj") for n in "qkv"], axis=2)
    p_qkv = p_qkv.reshape(16, NC, P, 384).transpose(0, 2, 1, 3).reshape(16, P, NC * 384)
    w_exp = np.concatenate([p_qkv, get("L0_ffn_o_proj")], axis=2)
    out = {
        "x_t": cont(get("x").reshape(B, T_IMG, C * XD).transpose(0, 2, 1)),
        "txt": cont(get("txt")),
        "ws_rep": cont(np.repeat(get("L0_tok_weighted_sum").T, XD, axis=0)),
        "w_rep": cont(np.tile(get("L0_tok_weight").T, (C, 1))),
        "w_qkv": cont(w_qkv),
        "b_qk": cont(b_qk),
        "b_v": cont(np.broadcast_to(get("L0_attn_bv"), (P, C))),
        "ident": np.eye(P, dtype=np.float32),
        "sim": cont(get("L0_ffn_sim_matrix")),
        "gates": cont(np.broadcast_to(get("L0_ffn_gates"), (P, 16))),
        "first": cont(np.broadcast_to(np.arange(16, 0, -1).astype(np.float32), (P, 16))),
        "w_exp": cont(w_exp),
        "w_o": cont(get("L0_attn_Wo").T),
        "b_o": cont(np.broadcast_to(get("L0_attn_bo"), (P, C))),
        "consts": cont(np.stack([np.eye(P), np.triu(np.full((P, P), MASKED), 1), np.tril(np.full((P, P), MASKED), -1)],
                                axis=1).astype(np.float32)),
    }
    return out


def build(nc, arrays, phases=3):
    a = {n: nc.dram_tensor(n, v.shape, mybir.dt.from_np(v.dtype), kind="ExternalInput").ap() for n, v in arrays.items()}
    out = nc.dram_tensor("out", [B, T, C], F32, kind="ExternalOutput").ap()
    scratch = {
        "h": nc.dram_tensor("s_h", [B, P, NT, C], F32, kind="Internal").ap(),
        "v": nc.dram_tensor("s_v", [B, P, NT, C], F32, kind="Internal").ap(),
        "pieces": nc.dram_tensor("s_pieces", [B, P, 4, PARTS, T], BF16, kind="Internal").ap(),
        "neg": nc.dram_tensor("s_neg", [8, 60, P], BF16, kind="Internal").ap(),
        "h2": nc.dram_tensor("s_h2", [B, P, NT, C], F32, kind="Internal").ap(),
    }
    if phases >= 1:
        front_phase(nc, a, scratch)
    if phases >= 2:
        attention_phase(nc, a, scratch, scratch["h2"])
    if phases >= 3:
        nc.disable_value_cache = True
        expert_phase(nc, a, scratch, out)


def kernel(**inputs):
    import concourse.bacc as bacc
    from concourse.bass_utils import run_bass_kernel_spmd

    arrays = layout(inputs)
    nc = bacc.Bacc("TRN2", target_bir_lowering=False, num_devices=1, dynamic_dma_scratch_size=1024)
    build(nc, arrays)
    return run_bass_kernel_spmd(nc, [arrays], core_ids=[0]).results[0]["out"]
```

```python
import concourse.bass as bass
from concourse import mybir
from contextlib import ExitStack

F32 = mybir.dt.float32
F32R = mybir.dt.float32r
BF16 = mybir.dt.bfloat16
ALU = mybir.AluOpType
ACT = mybir.ActivationFunctionType
AX = mybir.AxisListType

P = 128
B = 16
T_IMG, T_TXT = 512, 128
T = T_IMG + T_TXT
NT = T // P
C = 256
NC = C // P
XD = 4
KX = C * XD // P
HALF = T // 2
HEADS, DK = 16, 16
HPC = P // DK
PARTS = 3
EPS = 1e-5
MASKED = -1e30
BANK = 512


def front_phase(nc, a, scratch):
    ctx = ExitStack()
    with ctx:
        def sb(name, shape, dt=F32):
            return ctx.enter_context(nc.sbuf_tensor(name, shape, dt))

        def sem(name):
            return ctx.enter_context(nc.semaphore(name))

        stage_ws = sb("a_stage_ws", [P, KX, C])
        stage_w = sb("a_stage_w", [P, KX, C])
        tok_hi = sb("a_tok_hi", [P, KX, C], F32R)
        tok_lo = sb("a_tok_lo", [P, KX, C], F32R)
        stage_qkv = sb("a_stage_qkv", [P, 3, NC, C])
        qkv_hi = sb("a_qkv_hi", [P, 3, NC, C], F32R)
        qkv_lo = sb("a_qkv_lo", [P, 3, NC, C], F32R)
        bias_in = sb("a_bias_in", [P, 2, NC])
        bias_qk = sb("a_bias_qk", [P, 2, NC])
        ident = sb("a_ident", [P, P])
        x_in = sb("a_x_in", [P, 2, KX, T_IMG])
        x_hi = sb("a_x_hi", [P, KX, T_IMG], F32R)
        x_lo = sb("a_x_lo", [P, KX, T_IMG], F32R)
        h = sb("a_h", [P, 2, NT, C])
        stats = sb("a_stats", [P, NT, 6])
        mean_sum = sb("a_mean_sum", [P, NT, 2])
        mean_diff = sb("a_mean_diff", [P, NT, 1])
        mean = sb("a_mean", [P, NT, 1])
        spread = sb("a_spread", [P, NT, 1])
        var_eps = sb("a_var_eps", [P, NT, 1])
        minus_half = sb("a_minus_half", [P, NT, 1])
        var = sb("a_var", [P, NT, 1])
        rstd = sb("a_rstd", [P, NT, 1])
        xn = sb("a_xn", [P, NT, C])
        xt_hi = sb("a_xt_hi", [P, NC, T], F32R)
        xt_lo = sb("a_xt_lo", [P, NC, T], F32R)
        qk = sb("a_qk", [P, 4, T])
        rest = sb("a_rest", [P, 4, T])
        pieces = sb("a_pieces", [P, 2, 4, PARTS, T], BF16)
        v_out = sb("a_v_out", [P, 2, NT, C])

        tok_ps = ctx.enter_context(nc.psum_tensor("a_tok_ps", [P, 2, BANK], F32))
        xt_ps = ctx.enter_context(nc.psum_tensor("a_xt_ps", [P, 3 * BANK], F32))
        ring_ps = ctx.enter_context(nc.psum_tensor("a_ring_ps", [P, 3, BANK], F32))

        tok_loaded = sem("a_tok_loaded")
        loaded = sem("a_loaded")
        w_made = sem("a_w_made")
        half_set = sem("a_half_set")
        x_loaded = [sem(f"a_x_loaded{s}") for s in range(2)]
        x_high = sem("a_x_high")
        x_low = sem("a_x_low")
        tok_done = sem("a_tok_done")
        h_copied = sem("a_h_copied")
        txt_loaded = [sem(f"a_txt_loaded{s}") for s in range(2)]
        st_done = sem("a_st_done")
        ag_done = sem("a_ag_done")
        var_done = sem("a_var_done")
        rstd_done = sem("a_rstd_done")
        xn_done = sem("a_xn_done")
        xt_done = sem("a_xt_done")
        xt_high = sem("a_xt_high")
        xt_low = sem("a_xt_low")
        ring_qk = sem("a_ring_qk")
        qk_out = sem("a_qk_out")
        ring_v = sem("a_ring_v")
        v_copied = sem("a_v_copied")
        part1 = sem("a_part1")
        rest1 = sem("a_rest1")
        part2 = sem("a_part2")
        part3 = sem("a_part3")
        h_stored = sem("a_h_stored")
        stored = sem("a_stored")
        out_free = sem("a_out_free")

        STORES = 2
        tok_src = a["x_t"].rearrange("b (k p) t -> b p k t", p=P)
        block = ctx.enter_context(nc.Block())

        def loads(b, s):
            return 8 * (b - s) + 16

        def load_x(sp, b, s):
            sp.dma_start(x_in[:, s], tok_src[b]).then_inc(x_loaded[s], 16)

        @block.sync
        def _(sp):
            for dst, src in ((stage_ws[:], a["ws_rep"].rearrange("(k p) o -> p k o", p=P)),
                             (stage_w[:], a["w_rep"].rearrange("(k p) o -> p k o", p=P))):
                sp.dma_start(dst, src).then_inc(tok_loaded, 16)
            load_x(sp, 0, 0)
            for dst, src in ((stage_qkv[:], a["w_qkv"].rearrange("j (c p) o -> p j c o", p=P)),
                             (bias_in[:], a["b_qk"]), (ident[:], a["ident"])):
                sp.dma_start(dst, src).then_inc(loaded, 16)
            load_x(sp, 1, 1)
            sp.dma_start(h[:, 0, NT - 1, :], a["txt"][0]).then_inc(txt_loaded[0], 16)
            sp.dma_start(h[:, 1, NT - 1, :], a["txt"][1]).then_inc(txt_loaded[1], 16)

            sp.wait_ge(x_low, 4)
            load_x(sp, 2, 0)

            def step(b, s, more, load):
                sp.wait_ge(stored, 16 * STORES * b)
                sp.sem_inc(out_free, 1)
                if load:
                    sp.wait_ge(x_low, 4 * (b + 2))
                    load_x(sp, b + 3, 1 - s)
                sp.wait_ge(h_copied, 4 * (b + 1))
                sp.wait_ge(txt_loaded[s], loads(b, s))
                sp.dma_start(scratch["h"][b], h[:, s]).then_inc(h_stored, 16)
                sp.wait_ge(v_copied, NT * (b + 1))
                sp.dma_start(scratch["v"][b], v_out[:, s]).then_inc(stored, 16)
                if more:
                    sp.wait_ge(h_stored, 16 * (b + 1))
                    sp.wait_ge(xn_done, NT * (b + 1))
                    sp.dma_start(h[:, s, NT - 1, :], a["txt"][b + 2]).then_inc(txt_loaded[s], 16)
                sp.wait_ge(part1, 4 * (b + 1))
                sp.wait_ge(part2, 4 * (b + 1))
                sp.wait_ge(part3, 4 * (b + 1))
                sp.dma_start(scratch["pieces"][b].rearrange("u c p t -> p (u c) t"),
                             pieces[:, s].rearrange("p u c t -> p (u c) t")).then_inc(stored, 16)

            for s in range(2):
                step(s, s, True, True)
            with sp.Fori(1, B // 2 - 2) as i:
                for s in range(2):
                    step(2 * i + s, s, True, True)
            for b in range(B - 4, B):
                step(b, b % 2, b + 2 < B, b + 3 < B)
            sp.wait_ge(h_stored, 16 * B)
            sp.wait_ge(stored, 16 * STORES * B)

        @block.scalar
        def _(act):
            def h_out(b, s):
                act.wait_ge(txt_loaded[s], loads(b, s))
                for t in range(4):
                    act.wait_ge(tok_done, 4 * b + t + 1)
                    nc.scalar.copy(h[:, s, t, :], tok_ps[:, t % 2, 0:C]).then_inc(h_copied, 1)

            def transposed(b):
                act.wait_ge(xt_done, b + 1)
                nc.scalar.copy(xt_hi[:].rearrange("p c t -> p (c t)"), xt_ps[:, 0:NC * T]).then_inc(xt_high, 1)

            def project(b, s):
                act.wait_ge(part3, 4 * b)
                act.wait_ge(out_free, b)
                for u in range(4):
                    for half in range(2):
                        n = 2 * u + half
                        act.wait_ge(ring_qk, 8 * b + n + 1)
                        nc.scalar.activation(qk[:, u, half * HALF:(half + 1) * HALF], ring_ps[:, n % 3, 0:HALF],
                                             ACT.Identity, bias=bias_qk[:, u // 2, u % 2:u % 2 + 1],
                                             scale=0.25 if u < 2 else 1.0).then_inc(qk_out, 1)
                    act.wait_ge(qk_out, 8 * b + 2 * u + 2)
                    nc.scalar.copy(pieces[:, s, u, 0], qk[:, u]).then_inc(part1, 1)
                for u in range(4):
                    act.wait_ge(rest1, 4 * b + u + 1)
                    nc.scalar.copy(pieces[:, s, u, 1], rest[:, u]).then_inc(part2, 1)

            h_out(0, 0)
            act.wait_ge(w_made, 6)

            def step(b, s, more):
                transposed(b)
                if more:
                    h_out(b + 1, 1 - s)
                project(b, s)

            for s in range(2):
                step(s, s, True)
            with act.Fori(1, B // 2 - 1) as i:
                for s in range(2):
                    step(2 * i + s, s, True)
            step(B - 2, 0, True)
            step(B - 1, 1, False)

        @block.vector
        def _(dve):
            dve.wait_ge(tok_loaded, 16 * 2)
            nc.vector.tensor_tensor(stage_ws[:], stage_ws[:], stage_w[:], ALU.mult).then_inc(w_made, 1)
            dve.wait_ge(w_made, 1)
            nc.vector.tensor_copy(tok_hi[:], stage_ws[:]).then_inc(w_made, 1)
            dve.wait_ge(w_made, 2)
            nc.vector.tensor_tensor(tok_lo[:], stage_ws[:], tok_hi[:].bitcast(F32), ALU.subtract).then_inc(w_made, 1)

            def other_weights():
                dve.wait_ge(loaded, 16 * 3)
                nc.vector.tensor_copy(qkv_hi[:], stage_qkv[:]).then_inc(w_made, 1)
                nc.vector.tensor_copy(bias_qk[:, 1], bias_in[:, 1]).then_inc(w_made, 1)
                nc.vector.tensor_scalar(bias_qk[:, 0], bias_in[:, 0], 0.25, None, ALU.mult).then_inc(w_made, 1)
                dve.wait_ge(w_made, 6)
                nc.vector.tensor_tensor(qkv_lo[:], stage_qkv[:], qkv_hi[:].bitcast(F32), ALU.subtract).then_inc(w_made, 1)

            def split(b, s, t):
                rows = slice(t * P, (t + 1) * P)
                if t == 0:
                    dve.wait_ge(x_loaded[s], loads(b, s))
                nc.vector.tensor_copy(x_hi[:, :, rows], x_in[:, s, :, rows]).then_inc(x_high, 1)
                dve.wait_ge(x_high, 4 * b + t + 1)
                nc.vector.tensor_tensor(x_lo[:, :, rows], x_in[:, s, :, rows], x_hi[:, :, rows].bitcast(F32),
                                        ALU.subtract).then_inc(x_low, 1)

            def norm(b, s, ahead):
                dve.wait_ge(xt_done, b)
                for t in range(NT):
                    if t < NT - 1:
                        dve.wait_ge(h_copied, 4 * b + t + 1)
                    else:
                        dve.wait_ge(txt_loaded[s], loads(b, s))
                    nc.vector.bn_stats(stats[:, t], h[:, s, t]).then_inc(st_done, 1)
                    if ahead and t < NT - 1:
                        split(b + 1, 1 - s, t)
                dve.wait_ge(st_done, NT * (b + 1))
                even, odd = stats[:, :, 0:3], stats[:, :, 3:6]
                nc.vector.tensor_tensor(mean_sum[:], even[:, :, 1:3], odd[:, :, 1:3], ALU.add).then_inc(ag_done, 1)
                nc.vector.tensor_tensor(mean_diff[:], even[:, :, 1:2], odd[:, :, 1:2], ALU.subtract).then_inc(ag_done, 1)
                dve.wait_ge(ag_done, 5 * b + 2)
                nc.vector.tensor_scalar(mean[:], mean_sum[:, :, 0:1], 0.5, None, ALU.mult).then_inc(ag_done, 1)
                nc.vector.scalar_tensor_tensor(out=spread[:], in0=mean_diff[:], scalar=0.25, in1=mean_diff[:],
                                               op0=ALU.mult, op1=ALU.mult).then_inc(ag_done, 1)
                dve.wait_ge(ag_done, 5 * b + 4)
                nc.vector.scalar_tensor_tensor(out=var[:], in0=mean_sum[:, :, 1:2], scalar=1.0 / C, in1=spread[:],
                                               op0=ALU.mult, op1=ALU.add).then_inc(ag_done, 1)
                dve.wait_ge(ag_done, 5 * b + 5)
                nc.vector.tensor_scalar(var_eps[:], var[:], EPS, None, ALU.add).then_inc(var_done, 1)
                dve.wait_ge(rstd_done, b + 1)
                for t in range(NT):
                    nc.vector.tensor_scalar(xn[:, t], h[:, s, t], mean[:, t, 0:1], rstd[:, t, 0:1],
                                            ALU.subtract, ALU.mult).then_inc(xn_done, 1)

            def transposed(b):
                dve.wait_ge(xt_high, b + 1)
                nc.vector.tensor_tensor(xt_lo[:].rearrange("p c t -> p (c t)"), xt_ps[:, 0:NC * T],
                                        xt_hi[:].rearrange("p c t -> p (c t)").bitcast(F32), ALU.subtract).then_inc(xt_low, 1)

            def values(b, s):
                dve.wait_ge(out_free, b)
                for t in range(NT):
                    dve.wait_ge(ring_v, NT * b + t + 1)
                    nc.vector.tensor_copy(v_out[:, s, t], ring_ps[:, (8 + t) % 3, 0:C]).then_inc(v_copied, 1)

            for t in range(NT - 1):
                split(0, 0, t)
            other_weights()
            norm(0, 0, True)

            def step(b, s, ahead):
                transposed(b)
                if ahead >= 1:
                    norm(b + 1, 1 - s, ahead >= 2)
                values(b, s)

            for s in range(2):
                step(s, s, 2)
            with dve.Fori(1, B // 2 - 1) as i:
                for s in range(2):
                    step(2 * i + s, s, 2)
            step(B - 2, 0, 1)
            step(B - 1, 1, 0)

        @block.gpsimd
        def _(pool):
            def inverse_root(b):
                pool.wait_ge(var_done, b + 1)
                nc.gpsimd.tensor_tensor(rstd[:], var_eps[:], minus_half[:], ALU.pow).then_inc(rstd_done, 1)

            def step(b, s, more):
                if more:
                    inverse_root(b + 1)
                for u in range(4):
                    pool.wait_ge(part1, 4 * b + u + 1)
                    nc.gpsimd.tensor_tensor(rest[:, u], qk[:, u], pieces[:, s, u, 0], ALU.subtract).then_inc(rest1, 1)
                for u in range(4):
                    pool.wait_ge(part2, 4 * b + u + 1)
                    nc.gpsimd.tensor_tensor(pieces[:, s, u, 2], rest[:, u], pieces[:, s, u, 1], ALU.subtract).then_inc(part3, 1)

            nc.gpsimd.memset(minus_half[:], -0.5).then_inc(half_set, 1)
            pool.wait_ge(half_set, 1)
            inverse_root(0)
            for s in range(2):
                step(s, s, True)
            with pool.Fori(1, B // 2 - 1) as i:
                for s in range(2):
                    step(2 * i + s, s, True)
            step(B - 2, 0, True)
            step(B - 1, 1, False)

        @block.tensor
        def _(pe):
            def tokens(b, s):
                for t in range(4):
                    pe.wait_ge(x_low, 4 * b + t + 1)
                    if t >= 2:
                        pe.wait_ge(h_copied, 4 * b + t - 1)
                    elif t == 0:
                        pe.wait_ge(h_copied, 4 * b)
                    rows = slice(t * P, (t + 1) * P)
                    out = tok_ps[:, t % 2, 0:C]
                    for k in range(KX):
                        nc.tensor.matmul(out, x_hi[:, k, rows], tok_hi[:, k], start=(k == 0), stop=False)
                        nc.tensor.matmul(out, x_hi[:, k, rows], tok_lo[:, k], start=False, stop=False)
                        last = nc.tensor.matmul(out, x_lo[:, k, rows], tok_hi[:, k], start=False, stop=(k == KX - 1))
                    last.then_inc(tok_done, 1)

            def transposes(b):
                pe.wait_ge(xn_done, NT * (b + 1))
                pe.wait_ge(xt_low, b)
                for c in range(NC):
                    for t in range(NT):
                        at = c * T + t * P
                        last = nc.tensor.transpose(xt_ps[:, at:at + P], xn[:, t, c * P:(c + 1) * P], ident[:])
                last.then_inc(xt_done, 1)

            def project(b):
                pe.wait_ge(xt_low, b + 1)
                pe.wait_ge(v_copied, NT * b)
                for u in range(4):
                    j, o = u // 2, slice(u % 2 * P, u % 2 * P + P)
                    for half in range(2):
                        n = 2 * u + half
                        cols = slice(half * HALF, (half + 1) * HALF)
                        if n >= 3:
                            pe.wait_ge(qk_out, 8 * b + n - 2)
                        out = ring_ps[:, n % 3, 0:HALF]
                        for c in range(NC):
                            nc.tensor.matmul(out, qkv_hi[:, j, c, o], xt_hi[:, c, cols], start=(c == 0), stop=False)
                            nc.tensor.matmul(out, qkv_hi[:, j, c, o], xt_lo[:, c, cols], start=False, stop=False)
                            last = nc.tensor.matmul(out, qkv_lo[:, j, c, o], xt_hi[:, c, cols], start=False, stop=(c == NC - 1))
                        last.then_inc(ring_qk, 1)
                for t in range(NT):
                    rows = slice(t * P, (t + 1) * P)
                    if t < 3:
                        pe.wait_ge(qk_out, 8 * b + 6 + t)
                    else:
                        pe.wait_ge(v_copied, NT * b + t - 2)
                    out = ring_ps[:, (8 + t) % 3, 0:C]
                    for c in range(NC):
                        nc.tensor.matmul(out, xt_hi[:, c, rows], qkv_hi[:, 2, c, :], start=(c == 0), stop=False)
                        nc.tensor.matmul(out, xt_hi[:, c, rows], qkv_lo[:, 2, c, :], start=False, stop=False)
                        last = nc.tensor.matmul(out, xt_lo[:, c, rows], qkv_hi[:, 2, c, :], start=False, stop=(c == NC - 1))
                    last.then_inc(ring_v, 1)

            pe.wait_ge(w_made, 3)
            tokens(0, 0)
            pe.wait_ge(w_made, 7)

            def step(b, s, more):
                transposes(b)
                if more:
                    tokens(b + 1, 1 - s)
                project(b)

            for s in range(2):
                step(s, s, True)
            with pe.Fori(1, B // 2 - 1) as i:
                for s in range(2):
                    step(2 * i + s, s, True)
            step(B - 2, 0, True)
            step(B - 1, 1, False)


def attention_phase(nc, a, scratch, sink):
    ctx = ExitStack()
    with ctx:
        def sb(name, shape, dt=F32):
            return ctx.enter_context(nc.sbuf_tensor(name, shape, dt))

        def sem(name):
            return ctx.enter_context(nc.semaphore(name))

        GROUPS, GH = 4, 4
        SLOTS = 2 * GROUPS
        STACK = ((0, 0), (0, 1), (0, 2), (1, 0), (1, 1), (2, 0))
        ROWS = DK * len(STACK)
        RUNS = (((0, 0, 3, 1), (3, 1, 2, 1), (5, 2, 1, 1)), ((0, 0, 1, 3), (3, 0, 1, 2), (5, 0, 1, 1)))
        AT = {0: (0, 0), 2: (0, T), 1: (1, 0), 3: (1, 4 * P), 4: (1, 6 * P)}
        ROW_UNITS = (((NT - 1, 0, BANK, 0, NT - 1),),
                     ((NT - 1, BANK, T, 0, NT), (2, 0, 3 * P, P, 2)),
                     ((3, 0, 4 * P, 0, 3),),
                     ((1, 0, 2 * P, 0, 1), (0, 0, P, 2 * P, 0)))
        UNITS = len(ROW_UNITS)
        LOADS = len(RUNS[0]) + len(RUNS[1])
        TURNED = slice(3 * P, 3 * P + P // 2)
        PV = {(0, 1): (0, (0,)), (1, 0): (0, (1,)), (1, 1): (0, (2, 3)),
              (2, 1): (1, (0, 1)), (3, 0): (1, (2, 3)), (3, 1): (1, (4,))}
        WIDTH = (8 * P, 7 * P)
        E0 = (0, 8 * P)

        qs = sb("b_qs", [P, SLOTS, GH, T], BF16)
        ks = sb("b_ks", [P, SLOTS, GH, T], BF16)
        ex = sb("b_ex", [P, 2, GH, 15 * P])
        v_in = sb("b_v_in", [P, NT, C])
        v_pad = sb("b_v_pad", [P, 2, NT, HEADS, 2 * DK])
        h = sb("b_h", [P, 2, NT, C])
        ot = sb("b_ot", [P, 2, GROUPS, T])
        neg_max = sb("b_neg_max", [P, 2, GH, NT + 1])
        max_rest = sb("b_max_rest", [P, GH, NT])
        max_piece = sb("b_max_piece", [P, PARTS + 1, GH, NT], BF16)
        max_rows = sb("b_max_rows", [(PARTS + 1) * GH * NT, 2, P], BF16)
        rden = sb("b_rden", [P, HEADS])
        attn = sb("b_attn", [P, C])
        at_hi = sb("b_at_hi", [P, NC, P], F32R)
        at_lo = sb("b_at_lo", [P, NC, P], F32R)
        wo = ot[:, 0, 0, 0:NC * C].rearrange("p (c o) -> p c o", c=NC)
        wo_hi = sb("b_wo_hi", [P, NC, C], F32R)
        wo_lo = sb("b_wo_lo", [P, NC, C], F32R)
        bias_o = sb("b_bias_o", [P, C])
        bias_v = sb("b_bias_v", [P, C])
        consts = sb("b_consts", [P, 2, P])
        consts_bf = sb("b_consts_bf", [P, 2, P], BF16)
        idle = sb("b_idle", [P, 1])
        ident, ident_bf = consts[:, 0], consts_bf[:, 0]

        st_bank = ctx.enter_context(nc.psum_tensor("b_st_ps", [P, 2, 2 * BANK], F32))
        mx_bank = ctx.enter_context(nc.psum_tensor("b_mx_ps", [P, 2, BANK], F32))
        pv_bank = ctx.enter_context(nc.psum_tensor("b_pv_ps", [P, BANK], F32))
        tail_bank = ctx.enter_context(nc.psum_tensor("b_tail_ps", [P, BANK], F32))

        mask_loaded = sem("b_mask_loaded")
        const_loaded = sem("b_const_loaded")
        prep = sem("b_prep")
        filled = sem("b_filled")
        slot_loaded = [sem(f"b_slot_loaded{n}") for n in range(SLOTS)]
        neg_loaded = [sem(f"b_neg_loaded{n}") for n in range(SLOTS)]
        v_loaded = sem("b_v_loaded")
        h_loaded = [sem(f"b_h_loaded{s}") for s in range(2)]
        v_ready = sem("b_v_ready")
        h_ready = sem("b_h_ready")
        mx_done = sem("b_mx_done")
        mx_read = sem("b_mx_read")
        st_done = sem("b_st_done")
        exp_done = sem("b_exp_done")
        ex_masked = sem("b_ex_masked")
        pv_done = sem("b_pv_done")
        ot_out = sem("b_ot_out")
        piece_done = sem("b_piece_done")
        max_turned = sem("b_max_turned")
        rows_done = sem("b_rows_done")
        rows_stored = sem("b_rows_stored")
        o_turned = sem("b_o_turned")
        rden_done = sem("b_rden_done")
        attn_done = sem("b_attn_done")
        at_turned = sem("b_at_turned")
        at_high = sem("b_at_high")
        at_low = sem("b_at_low")
        proj_done = sem("b_proj_done")
        h2_done = sem("b_h2_done")
        h2_stored = sem("b_h2_stored")

        CUTS = 5

        block = ctx.enter_context(nc.Block())

        TAIL = {}
        for t in range(NT):
            TAIL[5 + 2 * t] = (0, t)
            TAIL[6 + 2 * t] = (1, t)

        def iterate(eng, step):
            step(-1, 1, False, True, False)
            step(0, 0, True, True, False)
            step(1, 1, True, True, True)
            with eng.Fori(1, B // 2 - 1) as i:
                step(2 * i, 0, True, True, True)
                step(2 * i + 1, 1, True, True, True)
            step(B - 2, 0, True, True, True)
            step(B - 1, 1, True, False, True)
            step(B, 0, False, False, True)

        def has_pv(g, cur, prev):
            return cur if g else prev

        def has_turn(g, cur, nxt):
            return nxt if g else cur

        @block.sync
        def _(sp):
            sp.dma_start(consts[:], a["consts"]).then_inc(mask_loaded, 16)

            def load_slot(b, g, n):
                chunk, first = g // 2, g % 2 * GH
                for side, stack in ((0, qs), (1, ks)):
                    src = scratch["pieces"][b, 2 * side + chunk].rearrange("c (d h) t -> c d h t", h=HPC)
                    for row, piece, copies, count in RUNS[side]:
                        part = src[piece:piece + count, :, first:first + GH].rearrange("c d h t -> c d (h t)")
                        if copies > 1:
                            part = part.broadcast_to([copies, DK, GH * T])
                        sp.dma_start(stack[row * DK:(row + copies * count) * DK, n].rearrange("r h t -> r (h t)"), part)\
                          .then_inc(slot_loaded[n], 16)

            def load_v(b):
                sp.dma_start(v_in[:], scratch["v"][b]).then_inc(v_loaded, 16)

            def load_h(b, s):
                sp.dma_start(h[:, s], scratch["h"][b]).then_inc(h_loaded[s], 16)

            load_slot(0, 0, 0)
            for dst, src in ((wo, a["w_o"].rearrange("(c p) o -> p c o", p=P)), (bias_o[:], a["b_o"]), (bias_v[:], a["b_v"])):
                sp.dma_start(dst, src).then_inc(const_loaded, 16)
            for n in range(1, SLOTS - 1):
                load_slot(n // GROUPS, n % GROUPS, n)
                if n == 1:
                    load_v(0)
            for s in range(2):
                load_h(s, s)

            def step(b, s, cur, nxt, prev):
                for g in range(GROUPS):
                    nb, ng, slot = (b + 1, 3, (1 - s) * GROUPS + 3) if g == 0 else (b + 2, g - 1, s * GROUPS + g - 1)
                    if cur and (nxt if g == 0 else nxt and not (isinstance(b, int) and b + 2 >= B)):
                        sp.wait_ge(st_done, 32 * b + 8 * g)
                        load_slot(nb, ng, slot)
                    if g == 1 and cur and nxt:
                        sp.wait_ge(v_ready, b + 1)
                        load_v(b + 1)
                    if has_turn(g, cur, nxt):
                        m = 4 * b + g + 3
                        slot = s * GROUPS + 3 if g == 0 else (1 - s) * GROUPS + g - 1
                        sp.wait_ge(rows_done, m + 1)
                        sp.dma_start(scratch["neg"][slot], max_rows[0:PARTS * GH * NT, (g + 1) % 2]).then_inc(rows_stored, 16)
                        sp.wait_ge(rows_stored, 16 * (m + 1))
                        sp.dma_start(qs[ROWS:ROWS + PARTS, slot],
                                     scratch["neg"][slot].rearrange("(j h t) q -> j h (t q)", j=PARTS, h=GH))\
                          .then_inc(neg_loaded[slot], 16)
                if prev:
                    sp.wait_ge(h2_done, NT * b)
                    sp.dma_start(sink[b - 1], h[:, 1 - s]).then_inc(h2_stored, 16)
                    if nxt:
                        sp.wait_ge(h2_stored, 16 * b)
                        load_h(b + 1, 1 - s)

            iterate(sp, step)
            sp.wait_ge(h2_stored, 16 * B)

        @block.gpsimd
        def _(pool):
            nc.gpsimd.memset(max_piece[:], 0.0).then_inc(filled, 1)
            pool.wait_ge(filled, 1)
            nc.gpsimd.memset(ks[ROWS:P], 1.0).then_inc(filled, 1)
            pool.wait_ge(filled, 2)
            nc.gpsimd.memset(v_pad[:], 1.0).then_inc(filled, 1)
            pool.wait_ge(filled, 3)
            nc.gpsimd.memset(idle[:], 0.0).then_inc(filled, 1)
            pool.wait_ge(filled, 4)
            pool.wait_ge(const_loaded, 16 * 3)

            def mask(b, g):
                pool.wait_ge(exp_done, 32 * b + 8 * g + 8)
                nc.gpsimd.tensor_tensor(idle[:], idle[:], idle[:], ALU.add)
                for kt in range(NT):
                    unit, col = AT[kt]
                    col += E0[unit]
                    blocks = ex[:, g % 2, :, col:col + P]
                    nc.gpsimd.affine_select(out=blocks, in_=blocks, compare_op=ALU.is_ge, fill=0.0, base=0,
                                            pattern=[[0, GH], [1, P]], channel_multiplier=-1).then_inc(ex_masked, 1)

            def values(b, s):
                if not (isinstance(b, int) and b < 2):
                    pool.wait_ge(pv_done, 8 * b - 8)
                pool.wait_ge(v_loaded, 16 * b + 16)
                for t in range(NT):
                    last = nc.gpsimd.tensor_tensor(v_pad[:, s, t, :, 0:DK], v_in[:, t].rearrange("p (h d) -> p h d", h=HEADS),
                                                   bias_v[:].rearrange("p (h d) -> p h d", h=HEADS), ALU.add)
                last.then_inc(v_ready, 1)

            def residual(b, s):
                pool.wait_ge(h_loaded[s], 8 * (b - s) + 16)
                for t in range(NT):
                    last = nc.gpsimd.tensor_tensor(h[:, s, t], h[:, s, t], bias_o[:], ALU.add)
                last.then_inc(h_ready, 1)

            def step(b, s, cur, nxt, prev):
                for g in range(GROUPS):
                    if cur:
                        mask(b, g)
                    if g == 1 and nxt:
                        values(b + 1, 1 - s)
                    if g == 2 and cur:
                        residual(b, s)

            iterate(pool, step)

        @block.scalar
        def _(act):
            def ot_copy(b, s, g, part):
                group, sg = 4 * b + g - 1, (s if g else 1 - s)
                cols = (slice(0, BANK), slice(BANK, T))[part]
                act.wait_ge(pv_done, 2 * group + part + 1)
                if isinstance(group, int) and group == 0 and part == 0:
                    act.wait_ge(prep, 3)
                if (g - 1) % GROUPS == 0 and part == 0 and not (isinstance(b, int) and b < 2):
                    act.wait_ge(o_turned, NT * (b - 1))
                nc.scalar.copy(ot[:, sg, (g - 1) % GROUPS, cols], pv_bank[:, 0:cols.stop - cols.start]).then_inc(ot_out, 1)

            def exponentials(b, r, unit):
                g, j = divmod(r, GH)
                act.wait_ge(st_done, 32 * b + 2 * r + unit + 1)
                if j == 0 and unit == 0 and not (isinstance(b, int) and 4 * b + g < 2):
                    act.wait_ge(pv_done, 2 * (4 * b + g) - 2)
                nc.scalar.activation(ex[:, g % 2, j, E0[unit]:E0[unit] + WIDTH[unit]],
                                     st_bank[:, unit, 0:WIDTH[unit]], ACT.Exp).then_inc(exp_done, 1)

            def step(b, s, cur, nxt, prev):
                for r in range(HEADS):
                    g, j = divmod(r, GH)
                    if j == 0 and g and has_pv(g - 1, cur, prev):
                        ot_copy(b, s, g - 1, 1)
                    if j == 0 and g == 0 and prev:
                        ot_copy(b - 1, 1 - s, 3, 1)
                    if j == 2 and has_pv(g, cur, prev):
                        ot_copy(b, s, g, 0)
                    if cur:
                        exponentials(b, r, 0)
                    if prev and r in TAIL and TAIL[r][0] == 0:
                        n = NT * (b - 1) + TAIL[r][1]
                        act.wait_ge(at_turned, n + 1)
                        nc.scalar.copy(at_hi[:].rearrange("p c t -> p (c t)"), tail_bank[:, 0:C]).then_inc(at_high, 1)
                    if cur:
                        exponentials(b, r, 1)

            iterate(act, step)

        @block.vector
        def _(dve):
            dve.wait_ge(mask_loaded, 16)
            nc.vector.tensor_copy(consts_bf[:], consts[:]).then_inc(prep, 1)
            dve.wait_ge(filled, 1)

            def row_maxima(b, r, unit):
                g, j = divmod(r, GH)
                dve.wait_ge(mx_done, HEADS * UNITS * b + UNITS * r + unit + 1)
                for _, k0, k1, col, to in ROW_UNITS[unit]:
                    last = nc.vector.tensor_reduce(neg_max[:, g % 2, j, to:to + 1], mx_bank[:, unit % 2, col:col + k1 - k0],
                                                   AX.X, ALU.max, negate=True)
                last.then_inc(mx_read, 1)

            def cut(m, g, n):
                src = neg_max[:, (g + 1) % 2, :, 0:NT]
                if n == 0:
                    dve.wait_ge(mx_read, GH * UNITS * (m + 1))
                else:
                    dve.wait_ge(piece_done, CUTS * m + n)
                if n == 0:
                    nc.vector.tensor_tensor(src[:, :, NT - 1:NT], src[:, :, NT - 1:NT], neg_max[:, (g + 1) % 2, :, NT:NT + 1],
                                            ALU.min).then_inc(piece_done, 1)
                if n == 1:
                    if not (isinstance(m, int) and m == 0):
                        dve.wait_ge(max_turned, m)
                    nc.vector.tensor_copy(max_piece[:, 0], src).then_inc(piece_done, 1)
                if n == 2:
                    nc.vector.tensor_tensor(max_rest[:], src, max_piece[:, 0], ALU.subtract).then_inc(piece_done, 1)
                if n == 3:
                    nc.vector.tensor_copy(max_piece[:, 1], max_rest[:]).then_inc(piece_done, 1)
                if n == 4:
                    nc.vector.tensor_tensor(max_piece[:, 2], max_rest[:], max_piece[:, 1], ALU.subtract).then_inc(piece_done, 1)

            def step(b, s, cur, nxt, prev):
                for r in range(HEADS):
                    g, j = divmod(r, GH)
                    m = 4 * b + g + 3
                    part, t = TAIL.get(r, (None, None)) if prev else (None, None)
                    turn = has_turn(g, cur, nxt)
                    n = NT * (b - 1) + t if part is not None else None
                    if part == 0:
                        turned = tail_bank[:].rearrange("p (h d) -> p h d", d=2 * DK)
                        dve.wait_ge(o_turned, n + 1)
                        nc.vector.reciprocal(rden[:], turned[:, :, DK]).then_inc(rden_done, 1)
                    if turn and j < 2:
                        cut(m, g, 4 * j)
                    if part == 0:
                        dve.wait_ge(rden_done, n + 1)
                        nc.vector.tensor_tensor(attn[:].rearrange("p (h d) -> p h d", d=DK), turned[:, :, 0:DK],
                                                rden[:].unsqueeze(2).broadcast_to([P, HEADS, DK]), ALU.mult)\
                          .then_inc(attn_done, 1)
                    if nxt:
                        row_maxima(b + 1, r, 0)
                    if turn and j == 0:
                        cut(m, g, 1)
                    if nxt:
                        row_maxima(b + 1, r, 1)
                    if turn and j == 0:
                        cut(m, g, 2)
                    if part == 1:
                        dve.wait_ge(proj_done, n + 1)
                        if t == 0:
                            dve.wait_ge(h_ready, b)
                        nc.vector.tensor_tensor(h[:, 1 - s, t], tail_bank[:, 0:C], h[:, 1 - s, t], ALU.add)\
                          .then_inc(h2_done, 1)
                    if nxt:
                        row_maxima(b + 1, r, 2)
                    if turn and j == 0:
                        cut(m, g, 3)
                    if part == 0:
                        dve.wait_ge(at_high, n + 1)
                        nc.vector.tensor_tensor(at_lo[:].rearrange("p c t -> p (c t)"), tail_bank[:, 0:C],
                                                at_hi[:].rearrange("p c t -> p (c t)").bitcast(F32), ALU.subtract)\
                          .then_inc(at_low, 1)
                    if turn and j == 1:
                        dve.wait_ge(max_turned, m + 1)
                    if nxt:
                        row_maxima(b + 1, r, 3)
                    if turn and j == 1:
                        if not (isinstance(m, int) and m < 2):
                            dve.wait_ge(rows_stored, 16 * (m - 1))
                        nc.vector.tensor_copy(max_rows[:, (g + 1) % 2], mx_bank[0:(PARTS + 1) * GH * NT, 1, TURNED].bitcast(BF16))\
                          .then_inc(rows_done, 1)
                    if isinstance(b, int) and b == -1 and r == GH:
                        dve.wait_ge(const_loaded, 16 * 3)
                        nc.vector.tensor_copy(wo_hi[:], wo).then_inc(prep, 1)
                        dve.wait_ge(prep, 2)
                        nc.vector.tensor_tensor(wo_lo[:], wo, wo_hi[:].bitcast(F32), ALU.subtract).then_inc(prep, 1)

            iterate(dve, step)

        @block.tensor
        def _(pe):
            pe.wait_ge(prep, 1)

            def rows_of_scores(b, s, r, unit):
                g, j = divmod(r, GH)
                slot = s * GROUPS + g
                if j == 0 and unit == 0:
                    pe.wait_ge(slot_loaded[slot], 8 * LOADS * (b - s) + 16 * LOADS)
                if not (isinstance(b, int) and UNITS * (HEADS * b + r) + unit < 2):
                    pe.wait_ge(mx_read, UNITS * (HEADS * b + r) + unit - 1)
                for qt, k0, k1, col, _ in ROW_UNITS[unit]:
                    diagonal = k1 == (qt + 1) * P
                    last = nc.tensor.matmul(mx_bank[:, unit % 2, col:col + k1 - k0], qs[0:ROWS, slot, j, qt * P:(qt + 1) * P],
                                            ks[0:ROWS, slot, j, k0:k1], start=True, stop=not diagonal)
                    if diagonal:
                        last = nc.tensor.matmul(mx_bank[:, unit % 2, col + k1 - k0 - P:col + k1 - k0], ident_bf, consts_bf[:, 1],
                                                start=False, stop=True)
                last.then_inc(mx_done, 1)

            def turned_scores(b, s, r, unit):
                g, j = divmod(r, GH)
                slot = s * GROUPS + g
                n = 32 * b + 2 * r + unit
                if j == 0 and unit == 0:
                    pe.wait_ge(neg_loaded[slot], 8 * (b - s) + 16)
                if not (isinstance(n, int) and n < 2):
                    pe.wait_ge(exp_done, n - 1)
                full = ROWS + PARTS
                for kt, (u, col) in AT.items():
                    if u != unit:
                        continue
                    width = T - kt * P
                    for q0 in range(0, width, BANK):
                        q1 = min(width, q0 + BANK)
                        last = nc.tensor.matmul(st_bank[:, unit, col + q0:col + q1], ks[0:full, slot, j, kt * P:(kt + 1) * P],
                                                qs[0:full, slot, j, kt * P + q0:kt * P + q1], start=True, stop=True)
                last.then_inc(st_done, 1)

            def weighted_values(b, s, g, chunk, tiles):
                group, sg, vg = 4 * b + g - 1, (g - 1) % 2, (s if g else 1 - s)
                heads = (g - 1) % GROUPS * GH
                if tiles[0] == 0:
                    if chunk == 0:
                        pe.wait_ge(v_ready, b + 1 if g else b)
                    if not (isinstance(group, int) and group == 0 and chunk == 0):
                        pe.wait_ge(ot_out, 2 * group + chunk)
                for kt in tiles:
                    unit, col = AT[kt]
                    col += E0[unit]
                    if chunk == 0 or kt == NT - 1:
                        pe.wait_ge(ex_masked, NT * group + kt + 1)
                    q0, q1 = ((kt * P, BANK), (BANK, T))[chunk]
                    last_kt = (NT - 2, NT - 1)[chunk]
                    for n in range(GH):
                        last = nc.tensor.matmul(pv_bank[2 * DK * n:2 * DK * (n + 1), q0 - chunk * BANK:q1 - chunk * BANK],
                                                v_pad[:, vg, kt, heads + n],
                                                ex[:, sg, n, col + q0 - kt * P:col + q1 - kt * P],
                                                start=(kt == 0), stop=(kt == last_kt))
                if tiles[-1] == last_kt:
                    last.then_inc(pv_done, 1)

            def step(b, s, cur, nxt, prev):
                for r in range(HEADS):
                    g, j = divmod(r, GH)
                    m = 4 * b + g + 3
                    part, t = TAIL.get(r, (None, None)) if prev else (None, None)
                    n = NT * (b - 1) + t if part is not None else None
                    if part == 0:
                        pe.wait_ge(ot_out, 8 * b)
                        if isinstance(n, int) and n == 0:
                            pe.wait_ge(prep, 3)
                        else:
                            pe.wait_ge(h2_done, n)
                        for u in range(GROUPS):
                            last = nc.tensor.transpose(tail_bank[:, u * P:(u + 1) * P],
                                                       ot[:, 1 - s, u, t * P:(t + 1) * P], ident)
                        last.then_inc(o_turned, 1)
                    if nxt:
                        rows_of_scores(b + 1, 1 - s, r, 0)
                    if cur:
                        if isinstance(b, int) and b == 0 and r == 0:
                            pe.wait_ge(filled, 2)
                        turned_scores(b, s, r, 0)
                    if part == 1:
                        pe.wait_ge(at_low, n + 1)
                        for c in range(NC):
                            nc.tensor.matmul(tail_bank[:, 0:C], at_hi[:, c], wo_hi[:, c], start=(c == 0), stop=False)
                            nc.tensor.matmul(tail_bank[:, 0:C], at_hi[:, c], wo_lo[:, c], start=False, stop=False)
                            last = nc.tensor.matmul(tail_bank[:, 0:C], at_lo[:, c], wo_hi[:, c], start=False, stop=(c == NC - 1))
                        last.then_inc(proj_done, 1)
                    if nxt:
                        if j == 2 and has_turn(g, cur, nxt):
                            pe.wait_ge(rows_done, m + 1)
                        rows_of_scores(b + 1, 1 - s, r, 1)
                    if (j, 0) in PV and has_pv(g, cur, prev):
                        weighted_values(b, s, g, *PV[j, 0])
                    if part == 0:
                        pe.wait_ge(attn_done, n + 1)
                        for c in range(NC):
                            last = nc.tensor.transpose(tail_bank[:, c * P:(c + 1) * P], attn[:, c * P:(c + 1) * P], ident)
                        last.then_inc(at_turned, 1)
                    if nxt:
                        rows_of_scores(b + 1, 1 - s, r, 2)
                    if cur:
                        turned_scores(b, s, r, 1)
                    if nxt:
                        rows_of_scores(b + 1, 1 - s, r, 3)
                    if j == 1 and has_turn(g, cur, nxt):
                        pe.wait_ge(piece_done, CUTS * (m + 1))
                        nc.tensor.transpose(mx_bank[0:(PARTS + 1) * GH * NT, 1, TURNED].bitcast(BF16),
                                            max_piece[:].rearrange("p j h t -> p (j h t)"), ident_bf).then_inc(max_turned, 1)
                    if (j, 1) in PV and has_pv(g, cur, prev):
                        weighted_values(b, s, g, *PV[j, 1])

            iterate(pe, step)


def expert_phase(nc, a, scratch, out):
    E, H = 16, 128
    W3 = 3 * H
    SCALE = 1.0 / float(H) ** 0.5
    LOW = -1e30
    OG = E // 2
    ctx = ExitStack()
    with ctx:
        def sb(name, shape, dt=F32):
            return ctx.enter_context(nc.sbuf_tensor(name, shape, dt))

        def sem(name):
            return ctx.enter_context(nc.semaphore(name))

        p_hi = sb("c_p_hi", [P, NC, E, W3], F32R)
        p_lo = sb("c_p_lo", [P, NC, E, W3], F32R)
        o_hi = sb("c_o_hi", [P, E, C], F32R)
        o_lo = sb("c_o_lo", [P, E, C], F32R)
        ident = sb("c_ident", [P, P])
        ones = sb("c_ones", [P, P])
        sim = sb("c_sim", [P, NC, E])
        sim_sq = sb("c_sim_sq", [P, NC, E])
        sim_ss = sb("c_sim_ss", [P, E])
        sim_rn = sb("c_sim_rn", [P, E])
        sim_n = sb("c_sim_n", [P, NC, E])
        sim_hi = sb("c_sim_hi", [P, NC, E], F32R)
        sim_lo = sb("c_sim_lo", [P, NC, E], F32R)
        gates = sb("c_gates", [P, E])
        gate_e = sb("c_gate_e", [P, E])
        gate_1 = sb("c_gate_1", [P, E])
        gate_s = sb("c_gate_s", [P, E])
        first = sb("c_first", [P, E])
        minus_half = sb("c_minus_half", [P, E])

        h_ln = sb("c_h_ln", [P, NT, C])
        h_res = sb("c_h_res", [P, NT, C])
        stats = sb("c_stats", [P, NT, 6])
        sums = sb("c_sums", [P, NT, 2])
        diff = sb("c_diff", [P, NT, 1])
        mean = sb("c_mean", [P, NT, 1])
        spread = sb("c_spread", [P, NT, 1])
        var = sb("c_var", [P, NT, 1])
        var_eps = sb("c_var_eps", [P, NT, 1])
        rstd = sb("c_rstd", [P, NT, 1])
        xf = h_ln
        sq = sb("c_sq", [P, C])
        ssq = sb("c_ssq", [P, NT, 1])
        ssq_c = sb("c_ssq_c", [P, NT, 1])
        rnorm = sb("c_rnorm", [P, NT, 1])
        xt_hi = sb("c_xt_hi", [P, 2, NC, T], F32R)
        xt_lo = sb("c_xt_lo", [P, 2, NC, T], F32R)
        raw = sb("c_raw", [P, NT, E])
        logit = sb("c_logit", [P, NT, E])
        gated = sb("c_gated", [P, NT, E])
        hard = sb("c_hard", [P, NT, E])
        active = sb("c_active", [P, NT, 1])
        top = sb("c_top", [P, NT, 1])
        cand = sb("c_cand", [P, NT, E])
        rank = sb("c_rank", [P, NT, 1])
        hot1 = sb("c_hot1", [P, NT, E])
        hot2 = sb("c_hot2", [P, NT, E])
        left = sb("c_left", [P, NT, E])
        mask = sb("c_mask", [P, NT, E])
        gexp = sb("c_gexp", [P, NT, E])
        wsum = sb("c_wsum", [P, NT, 1])
        w = sb("c_w", [P, 2, NT, E])
        wn = sb("c_wn", [P, NT, E])
        qkv = sb("c_qkv", [P, 2, NT, W3])
        qkv_odd = sb("c_qkv_odd", [P, 2, W3])
        qk_hi = sb("c_qk_hi", [P, 2, T], F32R)
        qk_lo = sb("c_qk_lo", [P, 2, T], F32R)
        neg_max = sb("c_neg_max", [P, NT])
        bias = sb("c_bias", [P, NT])
        denom = sb("c_denom", [P, NT, 1])
        rden = sb("c_rden", [P, NT, 1])
        ex = sb("c_ex", [P, 2, T])
        ex_t = sb("c_ex_t", [P, NT, T])
        ot_hi = sb("c_ot_hi", [P, T], F32R)
        ot_lo = sb("c_ot_lo", [P, T], F32R)
        y_odd = sb("c_y_odd", [P, 2, C])
        STAGES, STAGE = 3, NC * W3 + C
        flat = ex_t[:].rearrange("p t k -> p (t k)")
        stage = [flat[:, n * STAGE:(n + 1) * STAGE] for n in range(STAGES)]
        stage_p = [x[:, 0:NC * W3].rearrange("p (c j) -> p c j", c=NC) for x in stage]
        stage_o = [x[:, NC * W3:STAGE] for x in stage]

        q_bank = ctx.enter_context(nc.psum_tensor("c_q_ps", [P, 3, BANK], F32))
        x_bank = ctx.enter_context(nc.psum_tensor("c_x_ps", [P, 2, BANK], F32))
        y_bank = ctx.enter_context(nc.psum_tensor("c_y_ps", [P, 2, BANK], F32))
        x_flat = x_bank[:].rearrange("p a c -> p (a c)")
        y_flat = y_bank[:].rearrange("p a c -> p (a c)")

        const_loaded = sem("c_const_loaded")
        set_up = sem("c_set_up")
        pool_up = sem("c_pool_up")
        gate_exp = sem("c_gate_exp")
        sim_sum = sem("c_sim_sum")
        stage_loaded = [sem(f"c_stage_loaded{n}") for n in range(STAGES)]
        w_high = sem("c_w_high")
        w_low = sem("c_w_low")
        o_low = sem("c_o_low")
        hl_loaded = sem("c_hl_loaded")
        hr_loaded = sem("c_hr_loaded")
        stat_done = sem("c_stat_done")
        var_step = sem("c_var_step")
        var_done = sem("c_var_done")
        rstd_done = sem("c_rstd_done")
        xf_done = sem("c_xf_done")
        ssq_done = sem("c_ssq_done")
        ssq_ready = sem("c_ssq_ready")
        rnorm_done = sem("c_rnorm_done")
        xf_turned = sem("c_xf_turned")
        xf_high = sem("c_xf_high")
        xf_low = sem("c_xf_low")
        logit_done = sem("c_logit_done")
        route = sem("c_route")
        gexp_done = sem("c_gexp_done")
        w_done = sem("c_w_done")
        q_done = sem("c_q_done")
        q_acc = sem("c_q_acc")
        qkv_done = sem("c_qkv_done")
        qk_turned = sem("c_qk_turned")
        qk_high = sem("c_qk_high")
        qk_low = sem("c_qk_low")
        s_done = sem("c_s_done")
        s_max = sem("c_s_max")
        bias_done = sem("c_bias_done")
        ex_done = sem("c_ex_done")
        ex_turned = sem("c_ex_turned")
        ex_out = sem("c_ex_out")
        rden_done = sem("c_rden_done")
        wn_done = sem("c_wn_done")
        ot_done = sem("c_ot_done")
        ot_high = sem("c_ot_high")
        ot_low = sem("c_ot_low")
        y_done = sem("c_y_done")
        y_acc = sem("c_y_acc")
        y_out = sem("c_y_out")
        y_stored = sem("c_y_stored")
        ROUTE, ROUTE_PARTS = 14, 4
        route_top = sem("c_route_top")
        mask_step = sem("c_mask_step")
        w_step = sem("c_w_step")

        block = ctx.enter_context(nc.Block())

        PIECES = [[] for _ in range(NT * E)]
        for n in range(2):
            PIECES[2 + 4 * n].append(("turn_qk", n))
        for t in range(NT):
            PIECES[15 + 4 * t].append(("turn_ex", t))
            PIECES[9 + 4 * t].append(("scores", t))
            PIECES[14 + 2 * t].append(("stats", t))
            PIECES[25 + 2 * t].append(("norm", t))
        for n in range(2):
            PIECES[34 + 4 * n].append(("values", n))
        for n in range(NT * OG):
            PIECES[NT * OG + n].append(("output", n))
        for c in range(NC):
            PIECES[47 + 6 * c].append(("turn_xf", c))
        for n in range(ROUTE_PARTS):
            PIECES[57 + 6 * n].append(("route", n))
        NEXT = ("stats", "norm", "turn_xf", "route")

        def iterate(eng, expert, piece):
            def run(b, s, attend, project, ahead):
                for p, pieces in enumerate(PIECES):
                    if project:
                        expert(b + 1, 1 - s, *divmod(p, E))
                    for kind, n in pieces:
                        if kind in NEXT:
                            if ahead:
                                piece(kind, b + 2, s, n)
                        elif attend:
                            piece(kind, b, s, n)

            run(-2, 0, False, False, True)
            run(-1, 1, False, True, True)
            run(0, 0, True, True, True)
            run(1, 1, True, True, True)
            with eng.Fori(1, B // 2 - 1) as i:
                run(2 * i, 0, True, True, True)
                run(2 * i + 1, 1, True, True, True)
            run(B - 2, 0, True, True, False)
            run(B - 1, 1, True, False, False)

        @block.sync
        def _(sp):
            sp.dma_start(h_ln[:], scratch["h2"][0]).then_inc(hl_loaded, 16)
            for dst, src in ((sim[:], a["sim"].rearrange("(c p) e -> p c e", p=P)), (gates[:], a["gates"]),
                             (ident[:], a["ident"]), (first[:], a["first"])):
                sp.dma_start(dst, src).then_inc(const_loaded, 16)
            for e in range(E):
                n = e % STAGES
                if e >= STAGES:
                    sp.wait_ge(w_low, e - STAGES + 1)
                    sp.wait_ge(o_low, e - STAGES + 1)
                sp.dma_start(stage[n], a["w_exp"][e]).then_inc(stage_loaded[n], 16)
            sp.dma_start(h_res[:], scratch["h2"][0]).then_inc(hr_loaded, 16)

            def step(b, load_ln, load_res):
                if load_ln:
                    sp.wait_ge(ssq_done, NT * (b + 3))
                    sp.wait_ge(xf_turned, NC * (b + 3))
                    sp.dma_start(h_ln[:], scratch["h2"][b + 3]).then_inc(hl_loaded, 16)
                if not (isinstance(b, int) and b < 0):
                    sp.wait_ge(y_out, NT * (b + 1))
                    sp.dma_start(out[b].rearrange("(t p) c -> p t c", p=P), h_res[:]).then_inc(y_stored, 16)
                    if load_res:
                        sp.wait_ge(y_stored, 16 * (b + 1))
                        sp.dma_start(h_res[:], scratch["h2"][b + 1]).then_inc(hr_loaded, 16)

            step(-2, True, False)
            step(-1, True, False)
            with sp.Fori(0, B - 3) as b:
                step(b, True, True)
            for b in range(B - 3, B):
                step(b, False, b + 1 < B)
            sp.wait_ge(y_stored, 16 * B)

        @block.gpsimd
        def _(pool):
            nc.gpsimd.memset(minus_half[:], -0.5).then_inc(pool_up, 1)
            pool.wait_ge(pool_up, 1)
            nc.gpsimd.memset(ones[:], 1.0).then_inc(pool_up, 1)

            def low_half(e):
                pool.wait_ge(w_high, e + 1)
                nc.gpsimd.tensor_tensor(o_lo[:, e], stage_o[e % STAGES], o_hi[:, e].bitcast(F32), ALU.subtract).then_inc(o_low, 1)

            def expert(b, s, t, e):
                if isinstance(b, int) and b == 0 and t == 0 and e + STAGES < E:
                    low_half(e + STAGES)
                if e == E - 1:
                    pool.wait_ge(q_acc, NT * E * b + E * (t + 1))
                    nc.gpsimd.tensor_tensor(qkv[:, s, t], qkv[:, s, t], qkv_odd[:, t % 2], ALU.add).then_inc(qkv_done, 1)

            def piece(kind, b, s, n):
                if kind == "stats" and n == NT - 1:
                    pool.wait_ge(var_done, b + 1)
                    nc.gpsimd.tensor_tensor(rstd[:], var_eps[:], minus_half[:, 0:NT].unsqueeze(2), ALU.pow).then_inc(rstd_done, 1)
                if kind == "norm" and n == NT - 1:
                    pool.wait_ge(ssq_ready, b + 1)
                    nc.gpsimd.tensor_tensor(rnorm[:], ssq_c[:], minus_half[:, 0:NT].unsqueeze(2), ALU.pow).then_inc(rnorm_done, 1)
                    if isinstance(b, int) and b == 0:
                        pool.wait_ge(set_up, 2)
                        nc.gpsimd.tensor_tensor(sim_rn[:], sim_ss[:], minus_half[:], ALU.pow).then_inc(pool_up, 1)
                        for e in range(STAGES):
                            low_half(e)
                if kind == "output" and n % OG == OG - 1:
                    t = n // OG
                    pool.wait_ge(y_acc, NT * E * b + E * (t + 1))
                    nc.gpsimd.tensor_tensor(h_res[:, t], h_res[:, t], y_odd[:, t % 2], ALU.add).then_inc(y_out, 1)

            iterate(pool, expert, piece)

        @block.scalar
        def _(act):
            act.wait_ge(const_loaded, 64)
            nc.scalar.activation(gate_e[:], gates[:], ACT.Exp, scale=-1.0).then_inc(gate_exp, 1)

            def high_halves(e):
                act.wait_ge(stage_loaded[e % STAGES], 16 * (e // STAGES + 1))
                nc.scalar.copy(p_hi[:, :, e], stage_p[e % STAGES])
                nc.scalar.copy(o_hi[:, e], stage_o[e % STAGES]).then_inc(w_high, 1)

            for e in range(STAGES):
                high_halves(e)

            def expert(b, s, t, e):
                if isinstance(b, int) and b == 0 and t == 0 and e + STAGES < E:
                    high_halves(e + STAGES)

            def piece(kind, b, s, n):
                if kind == "turn_qk":
                    act.wait_ge(qk_turned, 2 * b + n + 1)
                    nc.scalar.copy(qk_hi[:, n], x_flat[:, 0:T]).then_inc(qk_high, 1)
                if kind == "scores":
                    act.wait_ge(bias_done, NT * b + n + 1)
                    act.wait_ge(ex_turned, NT * b + n - 1 if n else NT * b)
                    nc.scalar.activation(ex[:, n % 2].rearrange("p (a k) -> p a k", a=2), x_bank[:, :, 0:HALF], ACT.Exp,
                                         bias=bias[:, n:n + 1], scale=SCALE, accum_out=denom[:, n]).then_inc(ex_done, 1)
                if kind == "turn_ex":
                    act.wait_ge(ex_turned, NT * b + n + 1)
                    nc.scalar.copy(ex_t[:, :, n * P:(n + 1) * P],
                                   y_flat[:, 0:T].rearrange("p (t q) -> p t q", t=NT)).then_inc(ex_out, 1)
                if kind == "values":
                    act.wait_ge(ot_done, 2 * b + n + 1)
                    nc.scalar.copy(ot_hi[:, n * HALF:(n + 1) * HALF], y_bank[:, n, 0:HALF]).then_inc(ot_high, 1)
                if kind == "turn_xf":
                    act.wait_ge(xf_turned, NC * b + n + 1)
                    nc.scalar.copy(xt_hi[:, s, n], x_flat[:, 0:T]).then_inc(xf_high, 1)
                if kind == "route" and n == 0:
                    act.wait_ge(route, ROUTE * b + 3)
                    nc.scalar.activation(gexp[:], gated[:], ACT.Exp).then_inc(gexp_done, 1)

            iterate(act, expert, piece)

        @block.vector
        def _(dve):
            def router_weights(part):
                if part == 0:
                    dve.wait_ge(const_loaded, 64)
                    nc.vector.tensor_tensor(sim_sq[:], sim[:], sim[:], ALU.mult).then_inc(set_up, 1)
                if part == 1:
                    dve.wait_ge(sim_sum, 1)
                    nc.vector.tensor_scalar(sim_ss[:], x_bank[:, 0, 0:E], 1e-24, None, ALU.max).then_inc(set_up, 1)
                if part == 2:
                    dve.wait_ge(pool_up, 3)
                    nc.vector.tensor_tensor(sim_n[:], sim[:], sim_rn[:].unsqueeze(1).broadcast_to([P, NC, E]), ALU.mult)\
                      .then_inc(set_up, 1)
                    dve.wait_ge(gate_exp, 1)
                    nc.vector.tensor_scalar(gate_1[:], gate_e[:], 1.0, None, ALU.add).then_inc(set_up, 1)
                    dve.wait_ge(set_up, 4)
                    nc.vector.reciprocal(gate_s[:], gate_1[:]).then_inc(set_up, 1)
                    nc.vector.tensor_copy(sim_hi[:], sim_n[:]).then_inc(set_up, 1)
                    dve.wait_ge(set_up, 6)
                    nc.vector.tensor_tensor(sim_lo[:], sim_n[:], sim_hi[:].bitcast(F32), ALU.subtract).then_inc(set_up, 1)

            def low_halves(e):
                dve.wait_ge(w_high, e + 1)
                nc.vector.tensor_tensor(p_lo[:, :, e], stage_p[e % STAGES], p_hi[:, :, e].bitcast(F32), ALU.subtract)\
                  .then_inc(w_low, 1)

            def expert(b, s, t, e):
                n = NT * E * b + E * t + e
                acc = qkv_odd[:, t % 2] if e % 2 else qkv[:, s, t]
                if isinstance(b, int) and b == 0 and t == 0 and e + STAGES < E:
                    low_halves(e + STAGES)
                if e == 0:
                    if t == 0:
                        dve.wait_ge(w_done, b + 1)
                        dve.wait_ge(qkv_done, NT * b)
                    elif t >= 2:
                        dve.wait_ge(qkv_done, NT * b + t - 1)
                dve.wait_ge(q_done, n + 1)
                src = q_bank[:, (E * t + e) % 3, 0:W3]
                if e < 2:
                    nc.vector.tensor_scalar(acc, src, w[:, s, t, e:e + 1], None, ALU.mult).then_inc(q_acc, 1)
                else:
                    dve.wait_ge(q_acc, n - 1)
                    nc.vector.scalar_tensor_tensor(out=acc, in0=src, scalar=w[:, s, t, e:e + 1], in1=acc,
                                                   op0=ALU.mult, op1=ALU.add).then_inc(q_acc, 1)

            def router(b, s, part):
                def after(k):
                    dve.wait_ge(route, ROUTE * b + k)

                def wide(x):
                    return x[:].broadcast_to([P, NT, E])

                if part == 0:
                    dve.wait_ge(logit_done, b + 1)
                    dve.wait_ge(rnorm_done, b + 1)
                    nc.vector.tensor_tensor(raw[:], x_flat[:, 0:NT * E].rearrange("p (t e) -> p t e", e=E),
                                            wide(rnorm), ALU.mult).then_inc(route, 1)
                    after(1)
                    nc.vector.tensor_tensor(logit[:], raw[:], gate_s[:].unsqueeze(1).broadcast_to([P, NT, E]),
                                            ALU.subtract).then_inc(route, 1)
                    after(2)
                    nc.vector.tensor_scalar(gated[:], logit[:], 0.0, None, ALU.max).then_inc(route, 1)
                    nc.vector.tensor_scalar(hard[:], logit[:], 0.0, None, ALU.is_gt).then_inc(route, 1)
                    nc.vector.tensor_reduce(top[:], logit[:], AX.X, ALU.max).then_inc(route, 1)
                    after(5)
                    nc.vector.tensor_reduce(active[:], hard[:], AX.X, ALU.max).then_inc(mask_step, 1)
                if part == 1 or part == 2:
                    best, src, k = ((hot1, logit, 5), (hot2, left, 10))[part - 1]
                    nc.vector.tensor_tensor(best[:], src[:], wide(top), ALU.is_equal).then_inc(route, 1)
                    after(k + 1)
                    nc.vector.tensor_tensor(cand[:], best[:], first[:].unsqueeze(1).broadcast_to([P, NT, E]),
                                            ALU.mult).then_inc(route, 1)
                    after(k + 2)
                    nc.vector.tensor_reduce(rank[:], cand[:], AX.X, ALU.max).then_inc(route, 1)
                    after(k + 3)
                    nc.vector.tensor_tensor(best[:], cand[:], wide(rank), ALU.is_equal).then_inc(route, 1)
                    after(k + 4)
                if part == 1:
                    nc.vector.scalar_tensor_tensor(out=left[:], in0=hot1[:], scalar=LOW, in1=logit[:],
                                                   op0=ALU.mult, op1=ALU.add).then_inc(route, 1)
                    after(10)
                    nc.vector.tensor_reduce(top[:], left[:], AX.X, ALU.max).then_inc(route_top, 1)
                    dve.wait_ge(route_top, b + 1)
                if part < 3:
                    return
                nc.vector.tensor_tensor(cand[:], hot1[:], hot2[:], ALU.add).then_inc(mask_step, 1)
                dve.wait_ge(mask_step, 5 * b + 2)
                nc.vector.tensor_tensor(left[:], cand[:], wide(active), ALU.is_gt).then_inc(mask_step, 1)
                dve.wait_ge(mask_step, 5 * b + 3)
                nc.vector.tensor_tensor(mask[:], hard[:], left[:], ALU.max).then_inc(mask_step, 1)
                dve.wait_ge(mask_step, 5 * b + 4)
                dve.wait_ge(gexp_done, b + 1)
                nc.vector.tensor_tensor(cand[:], gexp[:], mask[:], ALU.mult).then_inc(mask_step, 1)
                dve.wait_ge(mask_step, 5 * b + 5)
                nc.vector.tensor_reduce(wsum[:], cand[:], AX.X, ALU.add).then_inc(w_step, 1)
                dve.wait_ge(w_step, 2 * b + 1)
                nc.vector.reciprocal(rank[:], wsum[:]).then_inc(w_step, 1)
                dve.wait_ge(w_step, 2 * b + 2)
                nc.vector.tensor_tensor(w[:, s], cand[:], wide(rank), ALU.mult).then_inc(w_done, 1)

            def piece(kind, b, s, n):
                if kind == "stats":
                    dve.wait_ge(hl_loaded, 16 * (b + 1))
                    nc.vector.bn_stats(stats[:, n], h_ln[:, n]).then_inc(stat_done, 1)
                if isinstance(b, int) and b == 0 and kind in NEXT:
                    if kind == "norm" and n == 0:
                        router_weights(0)
                    if kind == "turn_xf" and n == 0:
                        router_weights(1)
                        low_halves(0)
                    if kind == "route" and n == 0:
                        router_weights(2)
                    if kind == "route" and n in (1, 2):
                        low_halves(n)
                if kind == "stats" and n == NT - 1:
                    dve.wait_ge(stat_done, NT * (b + 1))
                    even, odd = stats[:, :, 0:3], stats[:, :, 3:6]
                    nc.vector.tensor_tensor(sums[:], even[:, :, 1:3], odd[:, :, 1:3], ALU.add).then_inc(var_step, 1)
                    nc.vector.tensor_tensor(diff[:], even[:, :, 1:2], odd[:, :, 1:2], ALU.subtract).then_inc(var_step, 1)
                    dve.wait_ge(var_step, 5 * b + 2)
                    nc.vector.tensor_scalar(mean[:], sums[:, :, 0:1], 0.5, None, ALU.mult).then_inc(var_step, 1)
                    nc.vector.scalar_tensor_tensor(out=spread[:], in0=diff[:], scalar=0.25, in1=diff[:],
                                                   op0=ALU.mult, op1=ALU.mult).then_inc(var_step, 1)
                    dve.wait_ge(var_step, 5 * b + 4)
                    nc.vector.scalar_tensor_tensor(out=var[:], in0=sums[:, :, 1:2], scalar=1.0 / C, in1=spread[:],
                                                   op0=ALU.mult, op1=ALU.add).then_inc(var_step, 1)
                    dve.wait_ge(var_step, 5 * b + 5)
                    nc.vector.tensor_scalar(var_eps[:], var[:], EPS, None, ALU.add).then_inc(var_done, 1)
                if kind == "norm":
                    if n == 0:
                        dve.wait_ge(rstd_done, b + 1)
                    nc.vector.tensor_scalar(xf[:, n], h_ln[:, n], mean[:, n, 0:1], rstd[:, n, 0:1],
                                            ALU.subtract, ALU.mult).then_inc(xf_done, 1)
                    dve.wait_ge(xf_done, NT * b + n + 1)
                    dve.wait_ge(ssq_done, NT * b + n)
                    nc.vector.tensor_tensor_reduce(out=sq[:], in0=xf[:, n], in1=xf[:, n], scale=1.0, scalar=0.0,
                                                   op0=ALU.mult, op1=ALU.add, accum_out=ssq[:, n]).then_inc(ssq_done, 1)
                if kind == "norm" and n == NT - 1:
                    dve.wait_ge(ssq_done, NT * (b + 1))
                    nc.vector.tensor_scalar(ssq_c[:], ssq[:], 1e-24, None, ALU.max).then_inc(ssq_ready, 1)
                if kind == "turn_xf":
                    dve.wait_ge(xf_high, NC * b + n + 1)
                    nc.vector.tensor_tensor(xt_lo[:, s, n], x_flat[:, 0:T], xt_hi[:, s, n].bitcast(F32),
                                            ALU.subtract).then_inc(xf_low, 1)
                if kind == "route":
                    router(b, s, n)
                if kind == "turn_qk":
                    dve.wait_ge(qk_high, 2 * b + n + 1)
                    nc.vector.tensor_tensor(qk_lo[:, n], x_flat[:, 0:T], qk_hi[:, n].bitcast(F32), ALU.subtract)\
                      .then_inc(qk_low, 1)
                if kind == "scores":
                    dve.wait_ge(s_done, NT * b + n + 1)
                    nc.vector.tensor_reduce(neg_max[:, n:n + 1], x_bank[:, :, 0:HALF], AX.XY, ALU.max, negate=True)\
                      .then_inc(s_max, 1)
                    dve.wait_ge(s_max, NT * b + n + 1)
                    nc.vector.tensor_scalar(bias[:, n:n + 1], neg_max[:, n:n + 1], SCALE, None, ALU.mult).then_inc(bias_done, 1)
                if kind == "values":
                    if n == 0:
                        dve.wait_ge(ex_done, NT * (b + 1))
                        nc.vector.reciprocal(rden[:], denom[:]).then_inc(rden_done, 1)
                        dve.wait_ge(rden_done, b + 1)
                        nc.vector.tensor_tensor(wn[:], w[:, s], rden[:].broadcast_to([P, NT, E]), ALU.mult)\
                          .then_inc(wn_done, 1)
                    dve.wait_ge(ot_high, 2 * b + n + 1)
                    cols = slice(n * HALF, (n + 1) * HALF)
                    nc.vector.tensor_tensor(ot_lo[:, cols], y_bank[:, n, 0:HALF], ot_hi[:, cols].bitcast(F32),
                                            ALU.subtract).then_inc(ot_low, 1)
                if kind == "output":
                    t = n // OG
                    if n == 0:
                        dve.wait_ge(wn_done, b + 1)
                        dve.wait_ge(hr_loaded, 16 * (b + 1))
                        dve.wait_ge(y_out, NT * b)
                    elif n % OG == 0 and t >= 2:
                        dve.wait_ge(y_out, NT * b + t - 1)
                    pair = n % OG
                    for e in range(2 * pair, 2 * pair + 2):
                        k = NT * E * b + E * t + e
                        src = y_bank[:, e // 2 % 2, e % 2 * C:(e % 2 + 1) * C]
                        acc = y_odd[:, t % 2] if e % 2 else h_res[:, t]
                        if e % 2 == 0:
                            dve.wait_ge(y_done, NT * OG * b + OG * t + e // 2 + 1)
                        if e == 1:
                            nc.vector.tensor_scalar(acc, src, wn[:, t, e:e + 1], None, ALU.mult).then_inc(y_acc, 1)
                        else:
                            if e > 1:
                                dve.wait_ge(y_acc, k - 1)
                            nc.vector.scalar_tensor_tensor(out=acc, in0=src, scalar=wn[:, t, e:e + 1], in1=acc,
                                                           op0=ALU.mult, op1=ALU.add).then_inc(y_acc, 1)

            iterate(dve, expert, piece)

        @block.tensor
        def _(pe):
            pe.wait_ge(set_up, 1)
            pe.wait_ge(pool_up, 2)
            for c in range(NC):
                last = nc.tensor.matmul(x_bank[:, 0, 0:E], ones[:], sim_sq[:, c], start=(c == 0), stop=(c == NC - 1))
            last.then_inc(sim_sum, 1)

            def expert(b, s, t, e):
                rows = slice(t * P, (t + 1) * P)
                n = E * t + e
                if n == 0:
                    pe.wait_ge(xf_low, NC * (b + 1))
                    pe.wait_ge(q_acc, NT * E * b)
                if isinstance(b, int) and b == 0 and t == 0:
                    pe.wait_ge(w_low, e + 1)
                if n >= 3:
                    pe.wait_ge(q_acc, NT * E * b + n - 2)
                dst = q_bank[:, n % 3, 0:W3]
                for c in range(NC):
                    nc.tensor.matmul(dst, xt_hi[:, s, c, rows], p_hi[:, c, e], start=(c == 0), stop=False)
                    nc.tensor.matmul(dst, xt_hi[:, s, c, rows], p_lo[:, c, e], start=False, stop=False)
                    last = nc.tensor.matmul(dst, xt_lo[:, s, c, rows], p_hi[:, c, e], start=False, stop=(c == NC - 1))
                last.then_inc(q_done, 1)

            def piece(kind, b, s, n):
                if kind == "turn_qk":
                    if n == 0:
                        pe.wait_ge(qkv_done, NT * (b + 1))
                        pe.wait_ge(w_done, b + 1)
                    else:
                        pe.wait_ge(qk_low, 2 * b + 1)
                    for t in range(NT):
                        last = nc.tensor.transpose(x_flat[:, t * P:(t + 1) * P], qkv[:, s, t, n * H:(n + 1) * H], ident[:])
                    last.then_inc(qk_turned, 1)
                if kind == "scores":
                    pe.wait_ge(qk_low, 2 * (b + 1))
                    pe.wait_ge(ex_done, NT * b + n)
                    for half in range(2):
                        dst, rows, cols = x_bank[:, half, 0:HALF], slice(n * P, (n + 1) * P), slice(half * HALF, (half + 1) * HALF)
                        nc.tensor.matmul(dst, qk_hi[:, 0, rows], qk_hi[:, 1, cols], start=True, stop=False)
                        nc.tensor.matmul(dst, qk_hi[:, 0, rows], qk_lo[:, 1, cols], start=False, stop=False)
                        last = nc.tensor.matmul(dst, qk_lo[:, 0, rows], qk_hi[:, 1, cols], start=False, stop=True)
                    last.then_inc(s_done, 1)
                if kind == "turn_ex":
                    if n == 0:
                        pe.wait_ge(y_acc, NT * E * b)
                    pe.wait_ge(ex_out, NT * b + n)
                    pe.wait_ge(ex_done, NT * b + n + 1)
                    for t in range(NT):
                        last = nc.tensor.transpose(y_flat[:, t * P:(t + 1) * P], ex[:, n % 2, t * P:(t + 1) * P], ident[:])
                    last.then_inc(ex_turned, 1)
                if kind == "values":
                    pe.wait_ge(ex_out, NT * (b + 1))
                    for t in range(NT):
                        last = nc.tensor.matmul(y_bank[:, n, 0:HALF], qkv[:, s, t, 2 * H:3 * H],
                                                ex_t[:, t, n * HALF:(n + 1) * HALF], start=(t == 0), stop=(t == NT - 1))
                    last.then_inc(ot_done, 1)
                if kind == "output":
                    t, pair = divmod(n, OG)
                    rows = slice(t * P, (t + 1) * P)
                    if n == 0:
                        if isinstance(b, int) and b == 0:
                            pe.wait_ge(o_low, E)
                        pe.wait_ge(ot_low, 2 * (b + 1))
                    if n >= 2:
                        pe.wait_ge(y_acc, NT * E * b + 2 * (n - 1))
                    dst = y_bank[:, n % 2]
                    hi = o_hi[:, 2 * pair:2 * pair + 2].rearrange("p e c -> p (e c)")
                    lo = o_lo[:, 2 * pair:2 * pair + 2].rearrange("p e c -> p (e c)")
                    nc.tensor.matmul(dst, ot_hi[:, rows], hi, start=True, stop=False)
                    nc.tensor.matmul(dst, ot_hi[:, rows], lo, start=False, stop=False)
                    nc.tensor.matmul(dst, ot_lo[:, rows], hi, start=False, stop=True).then_inc(y_done, 1)
                if kind == "turn_xf":
                    if isinstance(b, int) and b == 0:
                        pe.wait_ge(set_up, 2)
                    pe.wait_ge(xf_done, NT * (b + 1))
                    pe.wait_ge(xf_low, NC * b + n)
                    if not (isinstance(b, int) and b < 2):
                        pe.wait_ge(ex_done, NT * (b - 1))
                    for t in range(NT):
                        last = nc.tensor.transpose(x_flat[:, t * P:(t + 1) * P], xf[:, t, n * P:(n + 1) * P], ident[:])
                    last.then_inc(xf_turned, 1)
                if kind == "route" and n == 0:
                    if isinstance(b, int) and b == 0:
                        pe.wait_ge(set_up, 7)
                    pe.wait_ge(xf_low, NC * (b + 1))
                    for t in range(NT):
                        rows, dst = slice(t * P, (t + 1) * P), x_flat[:, t * E:(t + 1) * E]
                        for c in range(NC):
                            nc.tensor.matmul(dst, xt_hi[:, s, c, rows], sim_hi[:, c], start=(c == 0), stop=False)
                            nc.tensor.matmul(dst, xt_hi[:, s, c, rows], sim_lo[:, c], start=False, stop=False)
                            last = nc.tensor.matmul(dst, xt_lo[:, s, c, rows], sim_hi[:, c], start=False, stop=(c == NC - 1))
                    last.then_inc(logit_done, 1)

            iterate(pe, expert, piece)


def layout(inputs):
    import numpy as np

    def get(name):
        return np.asarray(inputs[name])

    def cont(v):
        return np.ascontiguousarray(v)

    order = np.arange(C).reshape(NC, HPC, DK).transpose(0, 2, 1).reshape(-1)
    w_qkv = np.stack([get("L0_attn_Wq").T[:, order], get("L0_attn_Wk").T[:, order], get("L0_attn_Wv").T])
    b_qk = np.stack([get("L0_attn_bq")[order].reshape(NC, P).T, get("L0_attn_bk")[order].reshape(NC, P).T], axis=1)
    p_qkv = np.concatenate([get(f"L0_ffn_{n}_proj") for n in "qkv"], axis=2)
    p_qkv = p_qkv.reshape(16, NC, P, 384).transpose(0, 2, 1, 3).reshape(16, P, NC * 384)
    w_exp = np.concatenate([p_qkv, get("L0_ffn_o_proj")], axis=2)
    out = {
        "x_t": cont(get("x").reshape(B, T_IMG, C * XD).transpose(0, 2, 1)),
        "txt": cont(get("txt")),
        "ws_rep": cont(np.repeat(get("L0_tok_weighted_sum").T, XD, axis=0)),
        "w_rep": cont(np.tile(get("L0_tok_weight").T, (C, 1))),
        "w_qkv": cont(w_qkv),
        "b_qk": cont(b_qk),
        "b_v": cont(np.broadcast_to(get("L0_attn_bv"), (P, C))),
        "ident": np.eye(P, dtype=np.float32),
        "sim": cont(get("L0_ffn_sim_matrix")),
        "gates": cont(np.broadcast_to(get("L0_ffn_gates"), (P, 16))),
        "first": cont(np.broadcast_to(np.arange(16, 0, -1).astype(np.float32), (P, 16))),
        "w_exp": cont(w_exp),
        "w_o": cont(get("L0_attn_Wo").T),
        "b_o": cont(np.broadcast_to(get("L0_attn_bo"), (P, C))),
        "consts": cont(np.stack([np.eye(P), np.triu(np.full((P, P), MASKED), 1)], axis=1).astype(np.float32)),
    }
    return out


def build(nc, arrays):
    a = {n: nc.dram_tensor(n, v.shape, mybir.dt.from_np(v.dtype), kind="ExternalInput").ap() for n, v in arrays.items()}
    out = nc.dram_tensor("out", [B, T, C], F32, kind="ExternalOutput").ap()
    scratch = {
        "h": nc.dram_tensor("s_h", [B, P, NT, C], F32, kind="Internal").ap(),
        "v": nc.dram_tensor("s_v", [B, P, NT, C], F32, kind="Internal").ap(),
        "pieces": nc.dram_tensor("s_pieces", [B, 4, PARTS, P, T], BF16, kind="Internal").ap(),
        "neg": nc.dram_tensor("s_neg", [8, 60, P], BF16, kind="Internal").ap(),
        "h2": nc.dram_tensor("s_h2", [B, P, NT, C], F32, kind="Internal").ap(),
    }
    front_phase(nc, a, scratch)
    attention_phase(nc, a, scratch, scratch["h2"])
    nc.disable_value_cache = True
    expert_phase(nc, a, scratch, out)


def kernel(**inputs):
    import concourse.bacc as bacc
    from concourse.bass_utils import run_bass_kernel_spmd

    arrays = layout(inputs)
    nc = bacc.Bacc("TRN2", target_bir_lowering=False, num_devices=1, dynamic_dma_scratch_size=1024)
    build(nc, arrays)
    return run_bass_kernel_spmd(nc, [arrays], core_ids=[0]).results[0]["out"]
```
